# Optimizing a Trainium2 kernel written in Bass

```python
import numpy as np
import jax
import jax.numpy as jnp

def _softmax(x, axis=-1):
    return jax.nn.softmax(x, axis=axis)

def _gelu(x):
    return jax.nn.gelu(x, approximate=True)

def _silu(x):
    return jax.nn.silu(x)

def _sigmoid(x):
    return jax.nn.sigmoid(x)

def _layernorm(x, axis=-1, eps=1e-05):
    m = jnp.mean(x, axis=axis, keepdims=True)
    v = jnp.var(x, axis=axis, keepdims=True)
    return (x - m) / jnp.sqrt(v + eps)

def _scatter_add(tgt, idx, src, axis=0):
    return tgt.at[idx].add(src)

def _segment_sum(src, seg, n):
    return jax.ops.segment_sum(src, seg, n)
kernel_name = 'mk_gnn_resnorm_d2_gnn_r32_5ffcd7'

def setup_inputs(seed: int=0):
    np.random.seed(seed)
    _w = jnp.asarray

    def _rec_inputs():
        import jax
        import jax.numpy as jnp
        _gk = jax.random.key(seed)
        x = -0.000202 + 1 * jax.random.normal(jax.random.fold_in(_gk, 1), (3125, 128), jnp.float32)
        _s = jax.random.randint(jax.random.fold_in(_gk, 2), (50000,), 0, 3125, jnp.int32)
        _d = jax.random.randint(jax.random.fold_in(_gk, 3), (50000,), 0, 3125, jnp.int32)
        _loop = jnp.arange(3125, dtype=jnp.int32)
        src = jnp.concatenate([_s, _d, _loop])
        dst = jnp.concatenate([_d, _s, _loop])
        _o = jnp.argsort(dst, stable=True)
        src = src[_o]
        dst = dst[_o]
        return (x, src, dst)
    x, src, dst = _rec_inputs()

    def _L0_gnn_setup():
        import jax, jax.numpy as jnp
        import numpy as np
        K = 3
        ALPHA = 0.5
        key = jax.random.key(seed)
        k1, k2, k3, k4 = jax.random.split(key, 4)
        N, E, D_IN, D_OUT = (50000, 20000, 128, 128)
        h = jax.random.normal(k1, (N, D_IN), dtype=jnp.float32)
        W = jax.random.normal(k2, (D_OUT, D_IN), dtype=jnp.float32) * (1.0 / np.sqrt(D_IN))
        src = jax.random.randint(k3, (E,), 0, N, dtype=jnp.int64)
        dst = jax.random.randint(k4, (E,), 0, N, dtype=jnp.int64)
        return {'h': h, 'W': W, 'src': src, 'dst': dst}
    _L0_gnn_all = _L0_gnn_setup()
    _L0_gnn_in = {k: v for k, v in _L0_gnn_all.items() if k in ('W',)}
    del _L0_gnn_all

    def _L1_gnn_setup():
        import jax, jax.numpy as jnp
        import numpy as np
        N_NODES = 50000
        N_EDGES = 25000
        H = 128
        LN_EPS = 1e-05
        key = jax.random.key(seed)
        ks = jax.random.split(key, 8)
        x = jax.random.normal(ks[0], (N_NODES, H), dtype=jnp.float32)
        edge_index = jax.random.randint(ks[1], (2, N_EDGES), 0, N_NODES, dtype=jnp.int64)
        W1 = jax.random.normal(ks[2], (2 * H, H), dtype=jnp.float32) * 0.02
        b1 = jnp.zeros((H,), dtype=jnp.float32)
        W2 = jax.random.normal(ks[3], (H, 1), dtype=jnp.float32) * 0.02
        b2 = jnp.zeros((1,), dtype=jnp.float32)
        gamma = jnp.ones((H,), dtype=jnp.float32)
        beta = jnp.zeros((H,), dtype=jnp.float32)
        return {'x': x, 'edge_index': edge_index, 'W1': W1, 'b1': b1, 'W2': W2, 'b2': b2, 'gamma': gamma, 'beta': beta}
    _L1_gnn_all = _L1_gnn_setup()
    _L1_gnn_in = {k: v for k, v in _L1_gnn_all.items() if k in ('W1', 'b1', 'W2', 'b2', 'gamma', 'beta')}
    del _L1_gnn_all
    return {'x': x, 'src': src, 'dst': dst, 'L0_gnn_W': _L0_gnn_in['W'], 'L1_gnn_W1': _L1_gnn_in['W1'], 'L1_gnn_b1': _L1_gnn_in['b1'], 'L1_gnn_W2': _L1_gnn_in['W2'], 'L1_gnn_b2': _L1_gnn_in['b2'], 'L1_gnn_gamma': _L1_gnn_in['gamma'], 'L1_gnn_beta': _L1_gnn_in['beta']}

def reference(x, src, dst, L0_gnn_W, L1_gnn_W1, L1_gnn_b1, L1_gnn_W2, L1_gnn_b2, L1_gnn_gamma, L1_gnn_beta):
    import jax
    import jax.numpy as jnp

    def _L0_gnn_ref(h, W, src, dst):
        import jax, jax.numpy as jnp
        import numpy as np
        K = 3
        ALPHA = 0.5
        N = h.shape[0]
        ones = jnp.ones(src.shape[0], dtype=h.dtype)
        out_deg = jax.ops.segment_sum(ones, src, num_segments=N)
        in_deg = jax.ops.segment_sum(ones, dst, num_segments=N)
        norm_out = jnp.clip(out_deg, 1.0, None) ** (-0.5)
        norm_in = jnp.clip(in_deg, 1.0, None) ** (-0.5)
        h0 = h
        x = h
        for _ in range(K):
            msg = (x * norm_out[:, None])[src]
            agg = jax.ops.segment_sum(msg, dst, num_segments=N)
            x = (1.0 - ALPHA) * (agg * norm_in[:, None]) + ALPHA * h0
        return x @ W.T

    def _L1_gnn_ref(x, edge_index, W1, b1, W2, b2, gamma, beta):
        import jax, jax.numpy as jnp
        import numpy as np
        N_NODES = 50000
        N_EDGES = 25000
        H = 128
        LN_EPS = 1e-05
        src = edge_index[0]
        tgt = edge_index[1]
        edge_feat = jnp.concatenate([x[src], x[tgt]], axis=1)
        h = jax.nn.relu(edge_feat @ W1 + b1)
        w = jax.nn.sigmoid(h @ W2 + b2)[:, 0]
        agg = jax.ops.segment_sum(w[:, None] * x[src], tgt, num_segments=x.shape[0])
        attended = x + agg
        mu = jnp.mean(attended, axis=-1, keepdims=True)
        var = jnp.mean(jnp.square(attended - mu), axis=-1, keepdims=True)
        out = (attended - mu) * jax.lax.rsqrt(var + LN_EPS) * gamma + beta
        return out
    edge_index = jnp.stack([src, dst])
    x = _layernorm(x + _L0_gnn_ref(x, L0_gnn_W, src, dst), axis=-1)
    x = _layernorm(x + _L1_gnn_ref(x, edge_index, L1_gnn_W1, L1_gnn_b1, L1_gnn_W2, L1_gnn_b2, L1_gnn_gamma, L1_gnn_beta), axis=-1)
    return x

_drawn_inputs = setup_inputs


def setup_inputs(seed=0):
    import zlib

    import numpy as np

    out = dict(_drawn_inputs(seed))
    spreads = {'L1_gnn_b1': (0.0, 0.8), 'L1_gnn_gamma': (1.0, 0.2), 'L1_gnn_beta': (0.0, 0.1)}
    factors = {'L1_gnn_W1': 5.882, 'L1_gnn_W2': 5.657}
    for name, (base, spread) in spreads.items():
        noise = np.random.default_rng([zlib.crc32(name.encode()), seed]).standard_normal(out[name].shape)
        drawn = base * np.exp(spread * noise) if base else spread * noise
        out[name] = jnp.asarray(drawn.astype(out[name].dtype))
    for name, factor in factors.items():
        out[name] = (out[name] * factor).astype(out[name].dtype)
    return out
```

```python
import concourse.bass as bass
from concourse import mybir
from contextlib import ExitStack


def gnn_kernel(nc, x, src, dst, w0, w1, b1, w2, b2, gamma, beta, out):
    f32, i32 = mybir.dt.float32, mybir.dt.int32
    f16, f8 = mybir.dt.float16, mybir.dt.float8e4
    ALU, ACT = mybir.AluOpType, mybir.ActivationFunctionType
    ET = mybir.EngineType

    P = 128
    N, D = x.shape
    E = src.shape[0]
    NB = -(-N // P)
    NPAD = NB * P
    JW = 20
    CODES = NB * JW
    TPB = 4
    BPS = 4
    TPS = TPB * BPS
    BE = TPB * P
    SB = -(-E // (TPS * P))
    T = SB * TPS
    NBAT = SB * BPS
    TB = -(-T // P)
    QR = P // BPS
    LN_EPS = 1e-5
    USCALE = 32.0
    NM = 8
    GROUP = 5
    assert D == P and CODES <= 512 and NB % 2 == 1 and SB % 2 == 1 and N + QR <= NPAD and SB >= 5

    ctx = ExitStack()
    with ctx:
        def sb(name, shape, dt):
            return ctx.enter_context(nc.sbuf_tensor(name, shape, dt))

        def sem(name):
            return ctx.enter_context(nc.semaphore(name))

        bank = [ctx.enter_context(nc.psum_tensor(f"bank{i}", [P, 512], f32)) for i in range(8)]

        src_table = nc.dram_tensor("src_table", (NPAD, 2 * D), f32, kind="Internal").ap()
        tgt_table = nc.dram_tensor("tgt_table", (NPAD, D), f32, kind="Internal").ap()

        xs = sb("xs", [P, NB, D], f32)
        hx_words = sb("hx", [P, max(NB * D, 3 * TB * P)], f32)
        hx = hx_words[:, 0:NB * D].rearrange("p (b k) -> p b k", k=D)
        ys_words = sb("ys", [P, max(NB * D, 2 * TB * P)], f32)
        ys = ys_words[:, 0:NB * D].rearrange("p (b k) -> p b k", k=D)
        UW = 2 * D + 2
        u0_words, u1_words = (sb(f"U{k}", [P, max(NB * UW // 2, 2 * TB * P)], f32) for k in range(2))
        U = [u[:, 0:NB * UW // 2].bitcast(f16).rearrange("p (b k) -> p b k", k=UW)
             for u in (u0_words, u1_words)]
        u8 = mybir.dt.uint8
        region = sb("region", [P, max(NB * NPAD // 4, 2 * TPS * 2 * D + 8192)], f32)
        count = region[:, 0:NB * NPAD // 4].bitcast(f8).rearrange("p (h d) -> p h d", h=NB)
        count_bytes = region[:, 0:NB * NPAD // 4].bitcast(u8).rearrange("p (h d) -> p h d", h=NB)

        def carve(block, taken, sizes, dt=f32):
            words = 1
            for n in sizes:
                words *= n
            view = block[:, taken[0]:taken[0] + words]
            taken[0] += words
            view = view.bitcast(dt) if dt != f32 else view
            if len(sizes) == 1:
                return view
            if len(sizes) == 2:
                return view.rearrange("p (a b) -> p a b", b=sizes[1])
            return view.rearrange("p (a b c) -> p a b c", b=sizes[1], c=sizes[2])

        taken = [0]
        G = carve(region, taken, [2 * TPS, 2 * D])
        dstb = [carve(region, taken, [BE], i32) for _ in range(2)]
        ohT = [carve(region, taken, [BE]) for _ in range(2)]
        qwin = [carve(region, taken, [D]) for _ in range(2)]
        ohJ = [carve(region, taken, [TPS, JW]) for _ in range(2)]
        S = [carve(region, taken, [TPB, D]) for _ in range(2)]
        fa = carve(region, taken, [GROUP, D])
        fb = carve(region, taken, [GROUP, D])
        res = [carve(region, taken, [GROUP, D]) for _ in range(2)]
        aggT = sb("aggT", [P, max(NPAD, 3 * TB * P)], f32)

        rows = carve(ys_words, [0], [2, TB, P], i32)
        ints = carve(u1_words, [0], [2, TB * P], i32)
        rowf = carve(hx_words, [0], [3, TB * P])
        colf = carve(aggT, [0], [3, TB * P])
        meta = sb("meta", [P, SB, 3, TPS], f32)
        jT = sb("jT", [P, T], f32)
        idxf = sb("idxf", [P, T], f32)
        idx = sb("idx", [P, T], i32)
        basebc = sb("basebc", [P, NBAT], f32)
        base = [sb(f"base{k}", [1, NBAT + 4], i32) for k in range(3)]
        rowid = sb("rowid", [P, SB], f32)
        shared_at = sb("shared_at", [1, NBAT + 4], i32)
        shared_is = sb("shared_is", [P, NBAT + 1], f32)
        step_f = sb("step_f", [P, NBAT], f32)
        column = sb("column", [P, NB, 1], f32)
        now = sb("now", [P, 3, TPS], f32)

        iota = sb("iota", [P, 512], f16)
        ident = sb("ident", [P, P], f32)
        ones = sb("ones", [1, P], f32)
        place = sb("place", [P, 1], f32)
        eps = sb("eps", [P, 1], f32)
        w0s = sb("w0s", [P, D], f32)
        w0T = sb("w0T", [P, D], f32)
        w1s = sb("w1s", [P, 2, D], f32)
        vec = sb("vec", [P, 4, D], f32)
        B1, W2, GAMMA, BETA = range(4)
        b2s = sb("b2s", [P, 1], f32)

        M = [sb(f"M{i}", [P, CODES], f16) for i in range(NM)]
        L = [sb(f"L{i}", [P, P], f16) for i in range(NM)]
        H = [sb(f"H{i}", [P, NM, NB], f16) for i in range(TPS // NM)]
        stage = [sb(f"stage{i}", [P, NB, JW], f8) for i in range(BPS)]
        deg = sb("deg", [P, NB], f32)
        rt = sb("rt", [P, NB], f32)
        nout = sb("nout", [P, NB], f32)
        su = sb("su", [P, NB], f32)
        sh = sb("sh", [P, NB], f32)
        indeg = sb("indeg", [P, NB], f32)
        irt = sb("irt", [P, NB], f32)
        nin = sb("nin", [P, NB], f32)
        c1 = sb("c1", [P, NB], f32)
        c3 = sb("c3", [P, NB], f32)
        t1 = [sb(f"t1{i}", [P, D], f32) for i in range(2)]
        t2 = [sb(f"t2{i}", [P, D], f32) for i in range(2)]
        x3T = sb("x3T", [P, D], f32)
        yT = sb("yT", [P, D], f32)
        yb = [sb(f"yb{i}", [P, D], f32) for i in range(2)]
        v = sb("v", [P, D], f32)
        bns = sb("bns", [P, 6], f32)
        mv = sb("mv", [P, 4], f32)
        Ps = [sb(f"Ps{i}", [P, D], f32) for i in range(2)]
        Qs = [sb(f"Qs{i}", [P, D], f32) for i in range(2)]
        inow = [sb(f"inow{i}", [P, TPS], i32) for i in range(2)]
        zs = [sb(f"zs{i}", [P, TPB], f32) for i in range(2)]
        ws = [sb(f"ws{i}", [P, TPB], f32) for i in range(2)]
        ohW = [sb(f"ohW{i}", [P, TPB, JW], f32) for i in range(2)]
        fbn = sb("fbn", [P, GROUP, 6], f32)
        fmv = sb("fmv", [P, GROUP, 2], f32)
        fsd = sb("fsd", [P, GROUP], f32)
        frs = sb("frs", [P, GROUP], f32)

        pads_set = sem("pads_set")
        idx_loaded = sem("idx_loaded")
        x_loaded = sem("x_loaded")
        w_loaded = sem("w_loaded")
        ident_zero = sem("ident_zero")
        consts_set = sem("consts_set")
        count_zeroed = sem("count_zeroed")
        rowf_ready = sem("rowf_ready")
        colf_psum = sem("colf_psum")
        colf_ready = sem("colf_ready")
        w0T_psum = sem("w0T_psum")
        base_psum = sem("base_psum")
        base_copied = sem("base_copied")
        base_ready = sem("base_ready")
        now_ready = sem("now_ready")
        onehot_ready = sem("onehot_ready")
        hi_ready = sem("hi_ready")
        tile_done = sem("tile_done")
        carried = sem("carried")
        column_read = sem("column_read")
        staged = sem("staged")
        count_copied = sem("count_copied")
        outdeg_ready = sem("outdeg_ready")
        outroot_ready = sem("outroot_ready")
        u_ready = sem("u_ready")
        hop_psum = sem("hop_psum")
        hop_drained = sem("hop_drained")
        indeg_ready = sem("indeg_ready")
        inroot_ready = sem("inroot_ready")
        x3T_psum = sem("x3T_psum")
        x3T_ready = sem("x3T_ready")
        v_psum = sem("v_psum")
        var_ready = sem("var_ready")
        dev_ready = sem("dev_ready")
        y_ready = sem("y_ready")
        yT_psum = sem("yT_psum")
        yT_ready = sem("yT_ready")
        pq_psum = sem("pq_psum")
        p_ready = sem("p_ready")
        q_ready = sem("q_ready")
        y_tabled = [sem(f"y_tabled{i}") for i in range(2)]
        y_kept = sem("y_kept")
        p_tabled = [sem(f"p_tabled{i}") for i in range(2)]
        q_tabled = [sem(f"q_tabled{i}") for i in range(2)]
        inow_ready = sem("inow_ready")
        gathered = [sem(f"gathered{i}") for i in range(2 * BPS)]
        win_loaded = [sem(f"win_loaded{i}") for i in range(2)]
        ohT_ready = sem("ohT_ready")
        s_psum = sem("s_psum")
        s_done = sem("s_done")
        z_ready = sem("z_ready")
        w_ready = sem("w_ready")
        ohw_ready = sem("ohw_ready")
        agg_psum = sem("agg_psum")
        sums_zeroed = sem("sums_zeroed")
        agg_added = sem("agg_added")
        att_psum = sem("att_psum")
        att_read = sem("att_read")
        fvar_ready = sem("fvar_ready")
        fdev_ready = sem("fdev_ready")
        res_ready = sem("res_ready")
        stored = [sem(f"stored{i}") for i in range(2)]
        chain = {n: sem(f"chain_{n}") for n in ("prep", "start", "hop0", "hop1", "hop2", "attend", "last")}

        block = ctx.enter_context(nc.Block())

        def chained(eng, name, before, length):
            done = [0]

            def link(ins=None):
                if ins is None:
                    assert done[0] == length, (name, done[0])
                    return
                done[0] += 1
                ins.then_inc(chain[name], 1)
                eng.wait_ge(chain[name], before + done[0])
            return link

        def load_four(engine, table, n, most):
            _, vals = nc.values_load_multi_w_load_instructions(
                table[0:1, bass.ds(n * BPS, BPS)], engines=[engine], min_val=0, max_val=most,
                skip_runtime_bounds_check_because="targets lie in 0..N-1, padding is N, places are clamped")
            return vals

        def in_pairs(eng, body, first, end, peeled=1):
            for n in range(first, first + peeled):
                body(n, n % 2)
            if end - first > peeled:
                with eng.Fori(first + peeled, end - 1, 2) as i:
                    body(i, 1)
                    body(i + 1, 0)

        def hold(eng, n):
            if not is_static(n):
                eng.nop(nofuse=True)

        def blk(a, b):
            return a[:, bass.ds(b, 1), :].rearrange("p o k -> p (o k)")

        def is_static(n):
            return isinstance(n, int)

        HALVES = [(0, min(4, TB))] + ([(4, TB)] if TB > 4 else [])
        GROUPS = [(g, min(g + GROUP, NB)) for g in range(0, NB, GROUP)]

        def stores(p, end):
            return 16 * sum((min(e, N // P) > a) + (min(e, N // P) < e)
                            for g, (a, e) in enumerate(GROUPS[:end]) if g % 2 == p)

        @block.sync
        def _(sp):
            whole, full = E // (P * P), (E % (P * P)) // P
            at = whole * P * P
            sp.wait_ge(pads_set, 2)
            for a, ap in enumerate((src, dst)):
                if whole:
                    sp.dma_start(rows[:, a, 0:whole, :], ap[0:at].rearrange("(b p i) -> p b i", p=P, i=P))\
                      .then_inc(idx_loaded, 16)
                if full:
                    sp.dma_start(rows[0:full, a, whole, :], ap[at:at + full * P].rearrange("(p i) -> p i", i=P))\
                      .then_inc(idx_loaded, 16)
                if E % P:
                    sp.dma_start(rows[full:full + 1, a, whole, 0:E % P],
                                 ap[at + full * P:E].rearrange("(p i) -> p i", p=1)).then_inc(idx_loaded, 16)
            whole = N // P
            sp.wait_ge(pads_set, 3)
            sp.dma_start(xs[:, 0:whole, :], x[0:whole * P, :].rearrange("(b p) k -> p b k", p=P))\
              .then_inc(x_loaded, 16)
            sp.dma_start(xs[0:N - whole * P, whole, :], x[whole * P:N, :]).then_inc(x_loaded, 16)
            sp.dma_start(w0s[:, :], w0).then_inc(w_loaded, 16)
            sp.dma_start(w1s[:, :, :], w1.rearrange("(a k) j -> k a j", a=2)).then_inc(w_loaded, 16)
            for i, a in enumerate((b1, w2.rearrange("k o -> (k o)"), gamma, beta)):
                sp.dma_start(vec[:, i, :], a.rearrange("(o k) -> o k", o=1).broadcast_to([P, D]))\
                  .then_inc(w_loaded, 16)
            sp.dma_start(b2s[:, :], b2.rearrange("(o k) -> o k", o=1).broadcast_to([P, 1]))\
              .then_inc(w_loaded, 16)

            def tables(b, p):
                sp.wait_ge(y_ready, b + 1)
                hold(sp, b)
                sp.dma_start(src_table[bass.ds(b * P, P), D:2 * D], yb[p][:, :]).then_inc(y_tabled[p], 16)
                sp.wait_ge(p_ready, b + 1)
                hold(sp, b)
                sp.dma_start(src_table[bass.ds(b * P, P), 0:D], Ps[p][:, :]).then_inc(p_tabled[p], 16)
                sp.wait_ge(q_ready, b + 1)
                hold(sp, b)
                sp.dma_start(tgt_table[bass.ds(b * P, P), :], Qs[p][:, :]).then_inc(q_tabled[p], 16)
            in_pairs(sp, tables, 0, NB)
            for p in range(2):
                sp.wait_ge(q_tabled[p], 16 * ((NB + 1 - p) // 2))

            def window(n, p):
                if not (is_static(n) and n < 2):
                    sp.wait_ge(ohT_ready, n - 1)
                    hold(sp, n)
                    sp.wait_ge(s_psum, (n - 1) * BPS)
                    hold(sp, n)
                first = load_four(ET.SP, base[0], n, N)
                for q in range(BPS):
                    sp.dma_start(qwin[p][q * QR:(q + 1) * QR, :], tgt_table[bass.ds(first[q], QR), :])\
                      .then_inc(win_loaded[p], 16)
                for q in range(BPS):
                    at = n * (BPS * BE) + q * BE
                    size = min(E - at, BE) if is_static(n) else BE
                    if size > 0:
                        sp.dma_start(dstb[p][q * QR:(q + 1) * QR, 0:size],
                                     dst[bass.ds(at, size)].rearrange("(o e) -> o e", o=1)
                                     .broadcast_to([QR, size])).then_inc(win_loaded[p], 16)
            in_pairs(sp, window, 0, SB - 2, 3)
            window(SB - 2, 1)
            window(SB - 1, 0)

            for g, (b0, b_end) in enumerate(GROUPS):
                sp.wait_ge(res_ready, g + 1)
                whole = min(b_end, N // P)
                if whole > b0:
                    sp.dma_start(out[b0 * P:whole * P, :].rearrange("(b p) k -> p b k", p=P),
                                 res[g % 2][:, 0:whole - b0, :]).then_inc(stored[g % 2], 16)
                if whole < b_end:
                    sp.dma_start(out[whole * P:N, :], res[g % 2][0:N - whole * P, whole - b0, :])\
                      .then_inc(stored[g % 2], 16)
            for p in range(min(2, len(GROUPS))):
                sp.wait_ge(stored[p], stores(p, len(GROUPS)))

        @block.gpsimd
        def _(g):
            nc.gpsimd.memset(rows[:, 0, E // (P * P):TB, :], NPAD).then_inc(pads_set, 1)
            nc.gpsimd.memset(rows[:, 1, E // (P * P):TB, :], N).then_inc(pads_set, 1)
            nc.gpsimd.memset(xs[:, NB - 1, :], 0.0).then_inc(pads_set, 1)
            nc.gpsimd.memset(ident[:, :], 0.0).then_inc(ident_zero, 1)
            nc.gpsimd.iota(iota[:, :], pattern=[[1, 512]], base=0, channel_multiplier=0,
                           allow_small_or_imprecise_dtypes=True)
            nc.gpsimd.memset(ones[:, :], 1.0)
            nc.gpsimd.memset(eps[:, :], LN_EPS)
            nc.gpsimd.iota(place[:, :], pattern=[[0, 1]], base=0, channel_multiplier=1,
                           allow_small_or_imprecise_dtypes=True)
            nc.gpsimd.memset(U[0][:, :, 2 * D:2 * D + 2], 1.0)
            g.wait_ge(ident_zero, 1)
            nc.gpsimd.affine_select(out=ident[:, :], in_=ident[:, :], compare_op=ALU.not_equal, fill=1.0,
                                    base=0, pattern=[[-1, P]], channel_multiplier=1).then_inc(consts_set, 1)
            nc.gpsimd.memset(region[:, 0:NB * NPAD // 4], 0.0).then_inc(count_zeroed, 1)

            g.wait_ge(base_ready, 1)
            g.wait_ge(count_zeroed, 1)

            def place_counts(n, p):
                first = load_four(ET.Pool, base[0], n, N)
                for q in range(BPS):
                    b = n * BPS + q
                    g.wait_ge(staged, b + 1)
                    if not (is_static(b) and b == 0):
                        g.wait_ge(count_copied, b)
                    nc.gpsimd.tensor_copy(count_bytes[:, :, bass.ds(first[q], JW)],
                                          stage[q][:, :, :].bitcast(u8)).then_inc(count_copied, 1)
            in_pairs(g, place_counts, 0, SB)
            nc.gpsimd.memset(aggT[:, 0:NPAD], 0.0).then_inc(sums_zeroed, 1)

            def keep_y(b, p):
                g.wait_ge(y_ready, b + 1)
                nc.gpsimd.tensor_copy(blk(ys, b), yb[p][:, :]).then_inc(y_kept, 1)
            in_pairs(g, keep_y, 0, NB)

            for p in range(2):
                g.wait_ge(p_tabled[p], 16 * ((NB + 1 - p) // 2))
                g.wait_ge(y_tabled[p], 16 * ((NB + 1 - p) // 2))

            def gather(n, p):
                if not (is_static(n) and n < 2):
                    for q in range(BPS):
                        g.wait_ge(gathered[p * BPS + q], 32 * (n - p))
                nc.gpsimd.tensor_copy(inow[p][:, :], idx[:, bass.ds(n * TPS, TPS)]).then_inc(inow_ready, 1)
                g.wait_ge(inow_ready, n + 1)
                for i in range(TPS):
                    q = i // TPB
                    if i % TPB == 0 and not (is_static(n) and n < 2):
                        g.wait_ge(agg_psum, (n - 2) * BPS + q + 1)
                        hold(g, n)
                    nc.gpsimd.indirect_dma_start(
                        out=G[:, p * TPS + i, :], out_offset=None, in_=src_table,
                        in_offset=bass.IndirectOffsetOnAxis(ap=inow[p][:, i:i + 1], axis=0))\
                        .then_inc(gathered[p * BPS + q], 16)
            gather(0, 0)
            gather(1, 1)
            in_pairs(g, gather, 2, SB)

        @block.vector
        def _(dve):
            link = chained(dve, "prep", 0, 9)
            dve.wait_ge(pads_set, 2)
            dve.wait_ge(idx_loaded, 16 * 2 * (bool(E // (P * P)) + bool((E % (P * P)) // P) + bool(E % P)))
            r = rows[:, :, :, :].rearrange("p a b i -> p a (b i)")
            nc.vector.tensor_single_scalar(ints[:, 0, :], r[:, 0, :], 7, ALU.logical_shift_right)
            nc.vector.tensor_copy(rowf[:, 2, :], r[:, 1, :])
            link(nc.vector.tensor_single_scalar(ints[:, 1, :], r[:, 0, :], P - 1, ALU.bitwise_and))
            nc.vector.tensor_copy(rowf[:, 0:2, :], ints[:, :, :]).then_inc(rowf_ready, 1)
            dve.wait_ge(colf_ready, 3 * len(HALVES))
            for k in range(0, 3, 2):
                nc.vector.memset(base[k][0:1, 0:4], 0)
                link(nc.vector.memset(base[k][0:1, NBAT:NBAT + 4], 0))
                nc.vector.tensor_copy(base[k][0:1, k:NBAT + k], colf[0:1, 2, 0:T:TPB])
            dve.wait_ge(base_copied, 1)
            nc.vector.memset(shared_at[0:1, :], 0)
            nc.vector.memset(shared_is[:, :], 0.0)
            link(nc.vector.tensor_tensor(step_f[:, 1:NBAT], basebc[:, 1:NBAT], basebc[:, 0:NBAT - 1],
                                         ALU.subtract))
            nc.vector.tensor_scalar(shared_is[:, 1:NBAT], step_f[:, 1:NBAT], float(JW - 1), None, ALU.is_le)
            nc.vector.tensor_scalar(shared_at[0:1, 2:NBAT + 1], step_f[0:1, 1:NBAT], float(JW - 1), 0.0,
                                    ALU.min, ALU.max)
            link(nc.vector.tensor_tensor(
                jT[:, :].rearrange("p (b t) -> p b t", t=TPB),
                colf[:, 2, 0:T].rearrange("p (b t) -> p b t", t=TPB),
                basebc[:, :].unsqueeze(2).broadcast_to([P, NBAT, TPB]), ALU.subtract))
            col = colf[:, :, 0:T].rearrange("p a (s t) -> p a s t", t=TPS)
            nc.vector.scalar_tensor_tensor(
                out=meta[:, :, 0, :], in0=col[:, 0], scalar=float(JW),
                in1=jT[:, :].rearrange("p (s t) -> p s t", t=TPS), op0=ALU.mult, op1=ALU.add)
            nc.vector.tensor_copy(meta[:, :, 1, :], col[:, 1])
            nc.vector.tensor_copy(meta[:, :, 2, :], col[:, 0])
            link(nc.vector.scalar_tensor_tensor(out=idxf[:, :], in0=colf[:, 0, 0:T], scalar=float(P),
                                                in1=colf[:, 1, 0:T], op0=ALU.mult, op1=ALU.add))
            nc.vector.tensor_scalar_min(idx[:, :], idxf[:, :], float(NPAD - 1)).then_inc(base_ready, 1)
            dve.wait_ge(base_ready, 1)
            dve.wait_ge(consts_set, 1)

            def carry(b, at, q):
                dve.wait_ge(tile_done, (b + 1) * TPB)
                dve.wait_ge(staged, b)
                own, before = (bank[k % BPS][:, 0:CODES].rearrange("p (h j) -> p h j", j=JW)
                               for k in (q, q - 1))
                nc.vector.tensor_scalar(column[:, :, :], before[:, :, bass.ds(at, 1)],
                                        shared_is[:, bass.ds(b, 1)], None, ALU.mult).then_inc(column_read, 1)
                dve.wait_ge(column_read, b)
                nc.vector.tensor_tensor(own[:, :, 0:1], own[:, :, 0:1], column[:, :, :], ALU.add)\
                  .then_inc(carried, 1)

            def onehots(n, p):
                if not (is_static(n) and n == 0):
                    dve.wait_ge(onehot_ready, n * TPS)
                nc.vector.tensor_copy(now[:, :, :], meta[:, bass.ds(n, 1), :, :].rearrange(
                    "p o a t -> p (o a) t")).then_inc(now_ready, 1)
                at = load_four(ET.DVE, shared_at, n, JW - 1)
                dve.wait_ge(now_ready, n + 1)
                for i in range(TPS):
                    t = n * TPS + i
                    if i % NM == 0:
                        if not (is_static(n) and n == 0):
                            dve.wait_ge(tile_done, t - TPS + NM)
                        nc.vector.tensor_tensor(
                            H[i // NM][:, :, :], iota[:, 0:NB].unsqueeze(1).broadcast_to([P, NM, NB]),
                            now[:, 2, i:i + NM].unsqueeze(2).broadcast_to([P, NM, NB]),
                            ALU.is_equal).then_inc(hi_ready, 1)
                    if not (is_static(n) and t < NM):
                        dve.wait_ge(tile_done, t - NM + 1)
                    nc.vector.tensor_scalar(M[i % NM][:, :], iota[:, 0:CODES], now[:, 0, i:i + 1], None,
                                            ALU.is_equal)
                    nc.vector.tensor_scalar(L[i % NM][:, :], iota[:, 0:P], now[:, 1, i:i + 1], None,
                                            ALU.is_equal).then_inc(onehot_ready, 1)
                    if i % TPB == 2 and not (is_static(n) and t < 2 * TPB):
                        q = i // TPB
                        carry(n * BPS + q - 1, at[q], (q - 1) % BPS)
            in_pairs(dve, onehots, 0, SB)
            at = load_four(ET.DVE, shared_at, SB, JW - 1)
            carry(NBAT - 1, at[0], BPS - 1)

            dve.wait_ge(tile_done, T)
            nc.vector.tensor_scalar_max(deg[:, :], bank[4][:, 0:NB], 1.0).then_inc(outdeg_ready, 1)
            dve.wait_ge(outroot_ready, 1)
            link(nc.vector.reciprocal(nout[:, :], rt[:, :]))
            nc.vector.tensor_scalar(su[:, :], nout[:, :], USCALE, None, ALU.mult)
            link(nc.vector.tensor_scalar(sh[:, :], nout[:, :], 0.5 * USCALE, None, ALU.mult))
            dve.wait_ge(x_loaded, 32)

            def start(b, p):
                link = chained(dve, "start", b * 1, 1)
                nc.vector.tensor_scalar(blk(hx, b), blk(xs, b), sh[:, bass.ds(b, 1)], None, ALU.mult)
                link(nc.vector.tensor_scalar(blk(U[0], b)[:, 0:D], blk(xs, b), su[:, bass.ds(b, 1)], None,
                                             ALU.mult))
                nc.vector.scalar_tensor_tensor(out=blk(U[0], b)[:, D:2 * D], in0=blk(xs, b),
                                               scalar=su[:, bass.ds(b, 1)], in1=blk(U[0], b)[:, 0:D],
                                               op0=ALU.mult, op1=ALU.subtract).then_inc(u_ready, 1)
            in_pairs(dve, start, 0, NB)

            def scaled_sums(k, b, p, factor, plus, link):
                ps = bank[2 * (k % 2) + p]
                link(nc.vector.scalar_tensor_tensor(
                    out=t1[p][:, :], in0=ps[:, D:2 * D], scalar=factor, in1=plus, op0=ALU.mult, op1=ALU.add))
                nc.vector.scalar_tensor_tensor(
                    out=t2[p][:, :], in0=ps[:, 0:D], scalar=factor, in1=t1[p][:, :], op0=ALU.mult,
                    op1=ALU.add).then_inc(hop_drained, 1)
                dve.wait_ge(hop_drained, k * NB + b + 1)

            def split(k, b, p, link):
                u = blk(U[(k + 1) % 2], b)
                link(nc.vector.tensor_copy(u[:, 0:D], t2[p][:, :]))
                nc.vector.tensor_tensor(u[:, D:2 * D], t2[p][:, :], u[:, 0:D], ALU.subtract)\
                  .then_inc(u_ready, 1)

            def hop0(b, p):
                link = chained(dve, "hop0", b * 4, 4)
                here = bass.ds(b, 1)
                dve.wait_ge(hop_psum, b + 1)
                nc.vector.tensor_scalar_max(indeg[:, here], bank[p][:, 2 * D:2 * D + 1], 1.0)\
                  .then_inc(indeg_ready, 1)
                dve.wait_ge(inroot_ready, b + 1)
                link(nc.vector.reciprocal(nin[:, here], irt[:, here]))
                nc.vector.tensor_scalar(c3[:, here], nin[:, here], 1.0 / USCALE, None, ALU.mult)
                link(nc.vector.scalar_tensor_tensor(out=c1[:, here], in0=nin[:, here], scalar=0.5,
                                                    in1=nout[:, here], op0=ALU.mult, op1=ALU.mult))
                scaled_sums(0, b, p, c1[:, here], blk(hx, b), link)
                split(0, b, p, link)
                link()

            def hop1(b, p):
                link = chained(dve, "hop1", b * 2, 2)
                dve.wait_ge(hop_psum, NB + b + 1)
                scaled_sums(1, b, p, c1[:, bass.ds(b, 1)], blk(hx, b), link)
                split(1, b, p, link)
                link()

            def hop2(b, p):
                link = chained(dve, "hop2", b * 4, 4)
                dve.wait_ge(hop_psum, 2 * NB + b + 1)
                scaled_sums(2, b, p, c3[:, bass.ds(b, 1)], blk(xs, b), link)
                dve.wait_ge(v_psum, b + 1)
                link(nc.vector.tensor_tensor(v[:, :], bank[5][:, 0:D], blk(xs, b), ALU.add))
                link(nc.vector.bn_stats(bns[:, :], v[:, :]))
                hold(dve, b)
                nc.vector.bn_aggr(mv[:, 0:2], bns[:, :]).then_inc(var_ready, 1)
                dve.wait_ge(dev_ready, b + 1)
                link(nc.vector.reciprocal(mv[:, 3:4], mv[:, 2:3]))
                if not (is_static(b) and b < 2):
                    dve.wait_ge(y_tabled[p], 8 * (b - p))
                    dve.wait_ge(y_kept, b - 1)
                nc.vector.tensor_scalar(yb[p][:, :], v[:, :], mv[:, 0:1], mv[:, 3:4], ALU.subtract, ALU.mult)\
                  .then_inc(y_ready, 1)
                dve.wait_ge(p_ready, b + 1)
                if not (is_static(b) and b < 2):
                    dve.wait_ge(q_tabled[p], 8 * (b - p))
                nc.vector.tensor_tensor(Qs[p][:, :], bank[6][:, D:2 * D], vec[:, B1, :], ALU.add)\
                  .then_inc(q_ready, 1)
                link()
            dve.wait_ge(w_loaded, 16 * 7)
            in_pairs(dve, hop0, 0, NB)
            in_pairs(dve, hop1, 0, NB)

            for q in range(BPS):
                nc.vector.tensor_scalar(rowid[q * QR:(q + 1) * QR, :], basebc[q * QR:(q + 1) * QR, q:NBAT:BPS],
                                        place[q * QR:(q + 1) * QR, 0:1], float(-q * QR), ALU.add, ALU.add)
            in_pairs(dve, hop2, 0, NB, 3)

            def scores(n, p, q, link):
                b = n * BPS + q
                dve.wait_ge(s_psum, b + 1)
                dve.wait_ge(gathered[p * BPS + q], 32 * (n - p) + 64)
                nc.vector.tensor_tensor(
                    S[q % 2][:, :, :], bank[q % 2][:, :].rearrange("p (t k) -> p t k", t=TPB),
                    G[:, p * TPS + q * TPB:p * TPS + (q + 1) * TPB, 0:D], ALU.add).then_inc(s_done, 1)
                dve.wait_ge(s_done, b + 1)
                for i in range(TPB):
                    z = nc.vector.scalar_tensor_tensor(
                        out=S[q % 2][:, i, :], in0=S[q % 2][:, i, :], scalar=0.0, in1=vec[:, W2, :],
                        op0=ALU.max, op1=ALU.mult, accum_out=zs[q % 2][:, i:i + 1])
                z.then_inc(z_ready, 1)
                dve.wait_ge(z_ready, b + 1)

            def weigh(n, p, q):
                b = n * BPS + q
                dve.wait_ge(w_ready, b + 1)
                if not (is_static(b) and b < 2):
                    dve.wait_ge(agg_psum, b - 1)
                nc.vector.tensor_tensor(
                    ohW[q % 2][:, :, :], ohJ[p][:, q * TPB:(q + 1) * TPB, :],
                    ws[q % 2][:, :].unsqueeze(2).broadcast_to([P, TPB, JW]), ALU.mult).then_inc(ohw_ready, 1)

            def add_sums(b, q, first_target):
                dve.wait_ge(agg_psum, b + 1)
                if is_static(b) and b == 0:
                    dve.wait_ge(sums_zeroed, 1)
                else:
                    dve.wait_ge(agg_added, b)
                at = aggT[:, bass.ds(first_target, JW)]
                nc.vector.tensor_tensor(at, bank[2 + q % 2][:, 0:JW], at, ALU.add).then_inc(agg_added, 1)

            def window_dmas(n, p):
                if is_static(n) and n == SB - 1:
                    some = BPS + -(-(E - n * BPS * BE) // BE)
                    return 16 * 2 * BPS * (n - p) // 2 + 16 * some
                return 16 * BPS * (n - p) + 32 * BPS
            def attend(n, p):
                begin = is_static(n) and n == 0
                first = load_four(ET.DVE, base[2], n, N)
                dve.wait_ge(win_loaded[p], window_dmas(n, p))
                if not (is_static(n) and n < 2):
                    dve.wait_ge(s_psum, (n - 1) * BPS)
                nc.vector.tensor_scalar(ohT[p][:, :], dstb[p][:, :], rowid[:, bass.ds(n, 1)], None,
                                        ALU.is_equal).then_inc(ohT_ready, 1)
                if not begin:
                    dve.wait_ge(ohw_ready, n * BPS - 1)
                nc.vector.tensor_tensor(
                    ohJ[p][:, :, :], iota[:, 0:JW].unsqueeze(1).broadcast_to([P, TPS, JW]),
                    jT[:, bass.ds(n * TPS, TPS)].unsqueeze(2).broadcast_to([P, TPS, JW]),
                    ALU.is_equal)
                for q in range(BPS):
                    scores(n, p, q, None)
                    if not (begin and q == 0):
                        weigh(*((n, p, q - 1) if q else (n - 1, 1 - p, BPS - 1)))
                    if not (begin and q < 2):
                        add_sums(n * BPS + q - 2, q, first[q])

            in_pairs(dve, attend, 0, SB - 2, 3)
            attend(SB - 2, 1)
            attend(SB - 1, 0)
            first = load_four(ET.DVE, base[2], SB, N)
            weigh(SB - 1, 0, BPS - 1)
            add_sums(NBAT - 2, 0, first[0])
            add_sums(NBAT - 1, 1, first[1])

            dve.wait_ge(y_kept, NB)
            done = [0]

            def last(ins):
                done[0] += 1
                ins.then_inc(chain["last"], 1)
                return done[0]
            for g, (b0, b_end) in enumerate(GROUPS):
                n = b_end - b0
                dve.wait_ge(att_psum, b_end)
                for i in range(n):
                    t = last(nc.vector.tensor_tensor(fa[:, i, :], bank[i][:, 0:D], ys[:, b0 + i, :], ALU.add))
                dve.wait_ge(chain["last"], t)
                for rnd in range(2):
                    source = fa if rnd == 0 else fb
                    for i in range(n):
                        t = last(nc.vector.bn_stats(fbn[:, i, :], source[:, i, :]))
                    dve.wait_ge(chain["last"], t)
                    for i in range(n):
                        z = nc.vector.bn_aggr(fmv[:, i, :], fbn[:, i, :])
                    z.then_inc(fvar_ready, 1)
                    dve.wait_ge(fdev_ready, 2 * g + rnd + 1)
                    t = last(nc.vector.reciprocal(frs[:, 0:n], fsd[:, 0:n]))
                    dve.wait_ge(chain["last"], t)
                    if rnd == 0:
                        for i in range(n):
                            t = last(nc.vector.tensor_scalar(fa[:, i, :], fa[:, i, :], fmv[:, i, 0:1],
                                                             frs[:, i:i + 1], ALU.subtract, ALU.mult))
                        dve.wait_ge(chain["last"], t)
                        t = last(nc.vector.tensor_tensor(fb[:, 0:n, :], fa[:, 0:n, :],
                                                         vec[:, GAMMA:GAMMA + 1, :].broadcast_to([P, n, D]),
                                                         ALU.mult))
                        dve.wait_ge(chain["last"], t)
                        t = last(nc.vector.tensor_tensor(fb[:, 0:n, :], fb[:, 0:n, :],
                                                         vec[:, BETA:BETA + 1, :].broadcast_to([P, n, D]),
                                                         ALU.add))
                        dve.wait_ge(chain["last"], t)
                        t = last(nc.vector.tensor_tensor(fb[:, 0:n, :], fb[:, 0:n, :], ys[:, b0:b_end, :],
                                                         ALU.add))
                        dve.wait_ge(chain["last"], t)
                    else:
                        if g >= 2:
                            dve.wait_ge(stored[g % 2], stores(g % 2, g))
                        for i in range(n):
                            z = nc.vector.tensor_scalar(res[g % 2][:, i, :], fb[:, i, :], fmv[:, i, 0:1],
                                                        frs[:, i:i + 1], ALU.subtract, ALU.mult)
                        z.then_inc(res_ready, 1)
                        dve.wait_ge(res_ready, g + 1)

        @block.tensor
        def _(pe):
            pe.wait_ge(rowf_ready, 1)
            pe.wait_ge(consts_set, 1)
            for a in range(3):
                for h, (k0, k1) in enumerate(HALVES):
                    for k in range(k0, k1):
                        z = nc.tensor.transpose(bank[2 * a + h][:, (k - k0) * P:(k - k0 + 1) * P],
                                                rowf[:, a, k * P:(k + 1) * P], ident[:, :])
                    z.then_inc(colf_psum, 1)
            pe.wait_ge(w_loaded, 16 * 7)
            nc.tensor.transpose(bank[7][:, 0:P], w0s[:, :], ident[:, :]).then_inc(w0T_psum, 1)
            pe.wait_ge(colf_ready, 3 * len(HALVES))
            nc.tensor.matmul(bank[6][:, 0:NBAT], ones[:, :], colf[0:1, 2, 0:T:TPB], start=True, stop=True)\
              .then_inc(base_psum, 1)

            def counts(n, p):
                begin, end = (is_static(n) and n == 0), (is_static(n) and n == SB - 1)
                for i in range(TPS):
                    t, q = n * TPS + i, i // TPB
                    if i % NM == 0:
                        pe.wait_ge(hi_ready, n * (TPS // NM) + i // NM + 1)
                    if i % TPB == 0 and not begin:
                        pe.wait_ge(staged, n * BPS + q - BPS + 1)
                        pe.wait_ge(carried, n * BPS + q - BPS + 1)
                    pe.wait_ge(onehot_ready, t + 1)
                    nc.tensor.matmul(bank[q][:, 0:CODES], L[i % NM][:, :], M[i % NM][:, :],
                                     start=i % TPB == 0, stop=i % TPB == TPB - 1)
                    nc.tensor.matmul(bank[4][:, 0:NB], L[i % NM][:, :], H[i // NM][:, i % NM, :],
                                     start=begin and i == 0, stop=end and i == TPS - 1).then_inc(tile_done, 1)
            counts(0, 0)
            with pe.Fori(1, SB - 3, 2) as n:
                counts(n, 1)
                counts(n + 1, 0)
            counts(SB - 2, 1)
            counts(SB - 1, 0)

            def node_step(step, b, p):
                if step == 0:
                    pe.wait_ge(hop_drained, 2 * NB + b + 1)
                    nc.tensor.transpose(bank[4][:, 0:P], t2[p][:, :], ident[:, :]).then_inc(x3T_psum, 1)
                elif step == 1:
                    pe.wait_ge(x3T_ready, b + 1)
                    nc.tensor.matmul(bank[5][:, 0:D], x3T[:, :], w0T[:, :], start=True, stop=True)\
                      .then_inc(v_psum, 1)
                elif step == 2:
                    pe.wait_ge(y_ready, b + 1)
                    nc.tensor.transpose(bank[7][:, 0:P], yb[p][:, :], ident[:, :]).then_inc(yT_psum, 1)
                else:
                    pe.wait_ge(yT_ready, b + 1)
                    if not (is_static(b) and b == 0):
                        pe.wait_ge(p_ready, b)
                        pe.wait_ge(q_ready, b)
                    nc.tensor.matmul(bank[6][:, 0:2 * D], yT[:, :],
                                     w1s[:, :, :].rearrange("k a j -> k (a j)"), start=True, stop=True)\
                      .then_inc(pq_psum, 1)

            def hop(k, b, p):
                begin = is_static(b) and b == 0
                width = 2 * D + 1 if k == 0 else 2 * D
                if b >= 2:
                    pe.wait_ge(hop_drained, k * NB + b - 1)
                after = [NB // 6, NB // 3, 2 * NB // 3, NB - 1]
                for h in range(NB):
                    if begin:
                        pe.wait_ge(u_ready, k * NB + h + 1)
                    z = nc.tensor.matmul(bank[2 * (k % 2) + p][:, 0:width],
                                         count[:, h, b * P:(b + 1) * P], U[k % 2][:, h, 0:width],
                                         start=h == 0, stop=h == NB - 1)
                    if h == NB - 1:
                        z.then_inc(hop_psum, 1)
                    for step in range(4):
                        if k == 2 and not begin and after[step] == h:
                            node_step(step, b - 1, 1 - p)
            pe.wait_ge(count_copied, NBAT)
            for k in range(3):
                for b in range(NB):
                    hop(k, b, b % 2)
            for step in range(4):
                node_step(step, NB - 1, (NB - 1) % 2)

            def target_part(n, p, q):
                b = n * BPS + q
                if q == 0:
                    pe.wait_ge(ohT_ready, n + 1)
                if not (is_static(b) and b < 2):
                    pe.wait_ge(s_done, b - 1)
                for i in range(TPB):
                    z = nc.tensor.matmul(bank[q % 2][:, i * P:(i + 1) * P],
                                         ohT[p][q * QR:(q + 1) * QR, i * P:(i + 1) * P],
                                         qwin[p][q * QR:(q + 1) * QR, :], start=True, stop=True)
                z.then_inc(s_psum, 1)

            def sums(n, p, q):
                b = n * BPS + q
                pe.wait_ge(ohw_ready, b + 1)
                if not (is_static(b) and b < 2):
                    pe.wait_ge(agg_added, b - 1)
                for i in range(TPB):
                    z = nc.tensor.matmul(bank[2 + q % 2][:, 0:JW], G[:, p * TPS + q * TPB + i, D:2 * D],
                                         ohW[q % 2][:, i, :], start=i == 0, stop=i == TPB - 1)
                z.then_inc(agg_psum, 1)

            def attend(n, p):
                for q in range(BPS):
                    target_part(n, p, q)
                    if not (is_static(n) and n == 0 and q < 2):
                        sums(*((n, p, q - 2) if q >= 2 else (n - 1, 1 - p, q + BPS - 2)))
            in_pairs(pe, attend, 0, SB)
            sums(SB - 1, 0, BPS - 2)
            sums(SB - 1, 0, BPS - 1)

            pe.wait_ge(agg_added, NBAT)
            for g, (b0, b_end) in enumerate(GROUPS):
                for b in range(b0, b_end):
                    if g:
                        pe.wait_ge(fvar_ready, 2 * g - 1)
                    nc.tensor.transpose(bank[b - b0][:, 0:P], aggT[:, b * P:(b + 1) * P], ident[:, :])\
                      .then_inc(att_psum, 1)

        @block.scalar
        def _(act):
            for a in range(3):
                for h, (k0, k1) in enumerate(HALVES):
                    act.wait_ge(colf_psum, a * len(HALVES) + h + 1)
                    nc.scalar.copy(colf[:, a, k0 * P:k1 * P], bank[2 * a + h][:, 0:(k1 - k0) * P])\
                      .then_inc(colf_ready, 1)
            act.wait_ge(base_psum, 1)
            nc.scalar.copy(basebc[:, :], bank[6][:, 0:NBAT]).then_inc(base_copied, 1)
            act.wait_ge(w0T_psum, 1)
            nc.scalar.mul(w0T[:, :], bank[7][:, 0:D], 0.5)

            def stage_counts(n, p):
                for q in range(BPS):
                    b = n * BPS + q
                    if not (is_static(b) and b == 0):
                        act.wait_ge(carried, b)
                    else:
                        act.wait_ge(tile_done, TPB)
                    if not (is_static(n) and n == 0):
                        act.wait_ge(count_copied, b - BPS + 1)
                    hold(act, n)
                    nc.scalar.activation(stage[q][:, :, :],
                                         bank[q][:, 0:CODES].rearrange("p (h j) -> p h j", j=JW),
                                         ACT.Copy, saturate=True).then_inc(staged, 1)
            in_pairs(act, stage_counts, 0, SB)

            act.wait_ge(outdeg_ready, 1)
            nc.scalar.sqrt(rt[:, :], deg[:, :]).then_inc(outroot_ready, 1)

            def in_root(b, p):
                act.wait_ge(indeg_ready, b + 1)
                nc.scalar.sqrt(irt[:, bass.ds(b, 1)], indeg[:, bass.ds(b, 1)]).then_inc(inroot_ready, 1)
            in_pairs(act, in_root, 0, NB)

            def node(b, p):
                act.wait_ge(x3T_psum, b + 1)
                nc.scalar.copy(x3T[:, :], bank[4][:, 0:P]).then_inc(x3T_ready, 1)
                act.wait_ge(var_ready, b + 1)
                nc.scalar.activation(mv[:, 2:3], mv[:, 1:2], ACT.Sqrt, bias=eps[:, 0:1]).then_inc(dev_ready, 1)
                act.wait_ge(yT_psum, b + 1)
                nc.scalar.copy(yT[:, :], bank[7][:, 0:P]).then_inc(yT_ready, 1)
                act.wait_ge(pq_psum, b + 1)
                if not (is_static(b) and b < 2):
                    act.wait_ge(p_tabled[p], 8 * (b - p))
                nc.scalar.copy(Ps[p][:, :], bank[6][:, 0:D]).then_inc(p_ready, 1)
            in_pairs(act, node, 0, NB, 3)

            def sigmoids(n, p):
                for q in range(BPS):
                    b = n * BPS + q
                    act.wait_ge(z_ready, b + 1)
                    if not (is_static(b) and b < 2):
                        act.wait_ge(ohw_ready, b - 1)
                    nc.scalar.activation(ws[q % 2][:, :], zs[q % 2][:, :], ACT.Sigmoid, bias=b2s[:, 0:1])\
                      .then_inc(w_ready, 1)
            in_pairs(act, sigmoids, 0, SB)

            for g, (b0, b_end) in enumerate(GROUPS):
                for rnd in range(2):
                    act.wait_ge(fvar_ready, 2 * g + rnd + 1)
                    nc.scalar.activation(fsd[:, 0:b_end - b0], fmv[:, 0:b_end - b0, 1], ACT.Sqrt,
                                         bias=eps[:, 0:1]).then_inc(fdev_ready, 1)


_INS = ["x", "src", "dst", "L0_gnn_W", "L1_gnn_W1", "L1_gnn_b1", "L1_gnn_W2", "L1_gnn_b2",
        "L1_gnn_gamma", "L1_gnn_beta"]


def kernel(**inputs):
    import numpy as _np
    import concourse.bacc as _bacc
    from concourse import mybir as _mybir
    from concourse.bass_utils import run_bass_kernel_spmd as _run

    nc = _bacc.Bacc("TRN2", target_bir_lowering=False, num_devices=1)
    arrays, args = {}, []
    for name in _INS:
        a = _np.ascontiguousarray(inputs[name])
        arrays[f"in_{name}_dram"] = a
        args.append(nc.dram_tensor(f"in_{name}_dram", a.shape, _mybir.dt.from_np(a.dtype), kind="ExternalInput").ap())
    shape = inputs["x"].shape
    args.append(nc.dram_tensor("out_0_dram", shape, _mybir.dt.float32, kind="ExternalOutput").ap())
    gnn_kernel(nc, *args)
    r = _run(nc, [arrays], core_ids=[0])
    return r.results[0]["out_0_dram"]
```

```python
import concourse.bass as bass
from concourse import mybir
from contextlib import ExitStack


def gnn_kernel(nc, x, src, dst, w0, w1, b1, w2, b2, gamma, beta, out):
    f32, i32 = mybir.dt.float32, mybir.dt.int32
    f16, f8 = mybir.dt.float16, mybir.dt.float8e4
    ALU, ACT = mybir.AluOpType, mybir.ActivationFunctionType
    ET = mybir.EngineType

    P = 128
    N, D = x.shape
    E = src.shape[0]
    NB = -(-N // P)
    NPAD = NB * P
    JW = 20
    CODES = NB * JW
    TPB = 4
    BPS = 4
    TPS = TPB * BPS
    BE = TPB * P
    SB = -(-E // (TPS * P))
    T = SB * TPS
    NBAT = SB * BPS
    TILES = -(-E // P)
    BATCHES = -(-TILES // TPB)
    TB = -(-T // P)
    QR = P // BPS
    LN_EPS = 1e-5
    USCALE = 32.0
    NM = 8
    GROUP = 5
    assert D == P and CODES <= 512 and NB % 2 == 1 and SB % 2 == 1 and N + QR <= NPAD and SB >= 5

    MAKER = "GGAGGGAGDGAGDGAG"
    PAIRS = ((2, 6), (10, 14))
    assert len(MAKER) == TPS and all(MAKER[i] == "A" for pair in PAIRS for i in pair)

    def tiles_in(n):
        return min(TPS, TILES - n * TPS) if isinstance(n, int) else TPS

    def tiles_of(b):
        return min(TPB, TILES - b * TPB) if isinstance(b, int) else TPB

    def batches_in(n):
        return min(BPS, BATCHES - n * BPS) if isinstance(n, int) else BPS

    def made(n, i):
        if MAKER[i] == "A":
            return n * len(PAIRS) + [i in pair for pair in PAIRS].index(True) + 1
        return n * MAKER.count(MAKER[i]) + MAKER[:i + 1].count(MAKER[i])

    ctx = ExitStack()
    with ctx:
        def sb(name, shape, dt):
            return ctx.enter_context(nc.sbuf_tensor(name, shape, dt))

        def sem(name):
            return ctx.enter_context(nc.semaphore(name))

        bank = [ctx.enter_context(nc.psum_tensor(f"bank{i}", [P, 512], f32)) for i in range(8)]

        src_table = nc.dram_tensor("src_table", (NPAD, 2 * D), f32, kind="Internal").ap()
        tgt_table = nc.dram_tensor("tgt_table", (NPAD, D), f32, kind="Internal").ap()

        xs = sb("xs", [P, NB, D], f32)
        hx_words = sb("hx", [P, max(NB * D, 3 * TB * P)], f32)
        hx = hx_words[:, 0:NB * D].rearrange("p (b k) -> p b k", k=D)
        ys_words = sb("ys", [P, max(NB * D, 2 * TB * P)], f32)
        ys = ys_words[:, 0:NB * D].rearrange("p (b k) -> p b k", k=D)
        UW = 2 * D + 2
        u0_words, u1_words = (sb(f"U{k}", [P, max(NB * UW // 2, 2 * TB * P + T)], f32) for k in range(2))
        U = [u[:, 0:NB * UW // 2].bitcast(f16).rearrange("p (b k) -> p b k", k=UW)
             for u in (u0_words, u1_words)]
        u8 = mybir.dt.uint8
        region = sb("region", [P, max(NB * NPAD // 4, 2 * TPS * 2 * D + 8192)], f32)
        count = region[:, 0:NB * NPAD // 4].bitcast(f8).rearrange("p (h d) -> p h d", h=NB)
        count_bytes = region[:, 0:NB * NPAD // 4].bitcast(u8).rearrange("p (h d) -> p h d", h=NB)

        def carve(block, taken, sizes, dt=f32):
            words = 1
            for n in sizes:
                words *= n
            view = block[:, taken[0]:taken[0] + words]
            taken[0] += words
            view = view.bitcast(dt) if dt != f32 else view
            if len(sizes) == 1:
                return view
            if len(sizes) == 2:
                return view.rearrange("p (a b) -> p a b", b=sizes[1])
            return view.rearrange("p (a b c) -> p a b c", b=sizes[1], c=sizes[2])

        taken = [0]
        G = carve(region, taken, [2 * TPS, 2 * D])
        dstb = [carve(region, taken, [BE], i32) for _ in range(2)]
        ohT = [carve(region, taken, [BE]) for _ in range(2)]
        qwin = [carve(region, taken, [D]) for _ in range(2)]
        ohJ = [carve(region, taken, [TPS, JW]) for _ in range(2)]
        S = [carve(region, taken, [TPB, D]) for _ in range(2)]
        fa = carve(region, taken, [GROUP, D])
        fb = carve(region, taken, [GROUP, D])
        res = [carve(region, taken, [GROUP, D]) for _ in range(2)]
        aggT = sb("aggT", [P, max(NPAD, 3 * TB * P)], f32)

        rows = carve(ys_words, [0], [2, TB, P], i32)
        ints = carve(u1_words, [0], [2, TB * P], i32)
        idxf = carve(u1_words, [2 * TB * P], [T])
        rowf = carve(hx_words, [0], [3, TB * P])
        colf = carve(aggT, [0], [3, TB * P])
        meta = sb("meta", [P, SB, 3, TPS], f32)
        CODE, LOW, HIGH = range(3)
        jT = sb("jT", [P, T], f32)
        idx = sb("idx", [P, T], i32)
        basebc = sb("basebc", [P, NBAT], f32)
        base = [sb(f"base{k}", [1, NBAT + 4], i32) for k in range(3)]
        rowid = sb("rowid", [P, SB], f32)
        shared_at = sb("shared_at", [1, NBAT + 4], i32)
        shared_is = sb("shared_is", [P, NBAT + 1], f32)
        step_f = sb("step_f", [P, NBAT], f32)
        column = sb("column", [P, NB, 1], f32)
        now = [sb(f"now{i}", [P, 3, TPS], f32) for i in range(2)]
        now_g = [sb(f"now_g{i}", [P, TPS], f32) for i in range(2)]
        now_a = [sb(f"now_a{i}", [P, TPS], f32) for i in range(2)]
        away = sb("away", [P, 2, P], f16)
        one = sb("one", [P, 1], f32)

        iota = sb("iota", [P, 512], f16)
        ident = sb("ident", [P, P], f32)
        ones = sb("ones", [1, P], f32)
        place = sb("place", [P, 1], f32)
        eps = sb("eps", [P, 1], f32)
        w0s = sb("w0s", [P, D], f32)
        w0T = sb("w0T", [P, D], f32)
        w1s = sb("w1s", [P, 2, D], f32)
        vec = sb("vec", [P, 4, D], f32)
        B1, W2, GAMMA, BETA = range(4)
        b2s = sb("b2s", [P, 1], f32)

        M = [sb(f"M{i}", [P, CODES], f16) for i in range(NM)]
        L = sb("L", [P, TPS, P], f16)
        H = [sb(f"H{i}", [P, NM, NB], f16) for i in range(TPS // NM)]
        stage = [sb(f"stage{i}", [P, NB, JW], f8) for i in range(2)]
        deg = sb("deg", [P, NB], f32)
        rt = sb("rt", [P, NB], f32)
        nout = sb("nout", [P, NB], f32)
        su = sb("su", [P, NB], f32)
        sh = sb("sh", [P, NB], f32)
        indeg = sb("indeg", [P, NB], f32)
        irt = sb("irt", [P, NB], f32)
        nin = sb("nin", [P, NB], f32)
        c1 = sb("c1", [P, NB], f32)
        c3 = sb("c3", [P, NB], f32)
        t1 = [sb(f"t1{i}", [P, D], f32) for i in range(2)]
        t2 = [sb(f"t2{i}", [P, D], f32) for i in range(2)]
        x3T = sb("x3T", [P, D], f32)
        yT = sb("yT", [P, D], f32)
        yb = [sb(f"yb{i}", [P, D], f32) for i in range(2)]
        v = sb("v", [P, D], f32)
        bns = sb("bns", [P, 6], f32)
        mv = sb("mv", [P, 4], f32)
        Ps = [sb(f"Ps{i}", [P, D], f32) for i in range(2)]
        Qs = [sb(f"Qs{i}", [P, D], f32) for i in range(2)]
        inow = [sb(f"inow{i}", [P, TPS], i32) for i in range(2)]
        zs = [sb(f"zs{i}", [P, TPB], f32) for i in range(2)]
        ws = [sb(f"ws{i}", [P, TPB], f32) for i in range(2)]
        ohW = [sb(f"ohW{i}", [P, TPB, JW], f32) for i in range(2)]
        fbn = sb("fbn", [P, GROUP, 6], f32)
        fmv = sb("fmv", [P, GROUP, 2], f32)
        fsd = sb("fsd", [P, GROUP], f32)
        frs = sb("frs", [P, GROUP], f32)

        pads_set = sem("pads_set")
        idx_loaded = sem("idx_loaded")
        x_loaded = sem("x_loaded")
        w_loaded = sem("w_loaded")
        ident_zero = sem("ident_zero")
        consts_set = sem("consts_set")
        count_zeroed = sem("count_zeroed")
        rowf_ready = sem("rowf_ready")
        colf_psum = sem("colf_psum")
        colf_ready = sem("colf_ready")
        w0T_psum = sem("w0T_psum")
        base_psum = sem("base_psum")
        base_copied = sem("base_copied")
        base_ready = sem("base_ready")
        now_ready = sem("now_ready")
        code_ready = sem("code_ready")
        low_ready = {maker: sem(f"low_ready_{maker}") for maker in "DGA"}
        now_g_ready = sem("now_g_ready")
        now_a_ready = sem("now_a_ready")
        away_ready = sem("away_ready")
        hi_ready = sem("hi_ready")
        tile_done = sem("tile_done")
        carried = sem("carried")
        column_read = sem("column_read")
        staged = sem("staged")
        count_copied = sem("count_copied")
        outdeg_ready = sem("outdeg_ready")
        outroot_ready = sem("outroot_ready")
        u_ready = sem("u_ready")
        hop_psum = sem("hop_psum")
        hop_drained = sem("hop_drained")
        indeg_ready = sem("indeg_ready")
        inroot_ready = sem("inroot_ready")
        x3T_psum = sem("x3T_psum")
        x3T_ready = sem("x3T_ready")
        v_psum = sem("v_psum")
        var_ready = sem("var_ready")
        dev_ready = sem("dev_ready")
        y_ready = sem("y_ready")
        yT_psum = sem("yT_psum")
        yT_ready = sem("yT_ready")
        pq_psum = sem("pq_psum")
        p_ready = sem("p_ready")
        q_ready = sem("q_ready")
        y_tabled = [sem(f"y_tabled{i}") for i in range(2)]
        y_kept = sem("y_kept")
        p_tabled = [sem(f"p_tabled{i}") for i in range(2)]
        q_tabled = [sem(f"q_tabled{i}") for i in range(2)]
        inow_ready = sem("inow_ready")
        gathered = [sem(f"gathered{i}") for i in range(2 * BPS)]
        win_loaded = [sem(f"win_loaded{i}") for i in range(2)]
        ohT_ready = sem("ohT_ready")
        s_psum = sem("s_psum")
        s_done = sem("s_done")
        z_ready = sem("z_ready")
        w_ready = sem("w_ready")
        ohw_ready = sem("ohw_ready")
        agg_psum = sem("agg_psum")
        sums_zeroed = sem("sums_zeroed")
        agg_added = sem("agg_added")
        att_psum = sem("att_psum")
        att_read = sem("att_read")
        fvar_ready = sem("fvar_ready")
        fdev_ready = sem("fdev_ready")
        res_ready = sem("res_ready")
        stored = [sem(f"stored{i}") for i in range(2)]
        chain = {n: sem(f"chain_{n}") for n in ("prep", "start", "hop0", "hop1", "hop2", "attend", "last")}

        block = ctx.enter_context(nc.Block())

        def chained(eng, name, before, length):
            done = [0]

            def link(ins=None):
                if ins is None:
                    assert done[0] == length, (name, done[0])
                    return
                done[0] += 1
                ins.then_inc(chain[name], 1)
                eng.wait_ge(chain[name], before + done[0])
            return link

        def load_four(engine, table, n, most):
            _, vals = nc.values_load_multi_w_load_instructions(
                table[0:1, bass.ds(n * BPS, BPS)], engines=[engine], min_val=0, max_val=most,
                skip_runtime_bounds_check_because="targets lie in 0..N-1, padding is N, places are clamped")
            return vals

        def in_pairs(eng, body, first, end, peeled=1):
            for n in range(first, first + peeled):
                body(n, n % 2)
            if end - first > peeled:
                with eng.Fori(first + peeled, end - 1, 2) as i:
                    body(i, 1)
                    body(i + 1, 0)

        def hold(eng, n):
            if not is_static(n):
                eng.nop(nofuse=True)

        def blk(a, b):
            return a[:, bass.ds(b, 1), :].rearrange("p o k -> p (o k)")

        def is_static(n):
            return isinstance(n, int)

        HALVES = [(0, min(4, TB))] + ([(4, TB)] if TB > 4 else [])
        GROUPS = [(g, min(g + GROUP, NB)) for g in range(0, NB, GROUP)]

        def stores(p, end):
            return 16 * sum((min(e, N // P) > a) + (min(e, N // P) < e)
                            for g, (a, e) in enumerate(GROUPS[:end]) if g % 2 == p)

        @block.sync
        def _(sp):
            whole, full = E // (P * P), (E % (P * P)) // P
            at = whole * P * P
            sp.wait_ge(pads_set, 2)
            for a, ap in enumerate((src, dst)):
                if whole:
                    sp.dma_start(rows[:, a, 0:whole, :], ap[0:at].rearrange("(b p i) -> p b i", p=P, i=P))\
                      .then_inc(idx_loaded, 16)
                if full:
                    sp.dma_start(rows[0:full, a, whole, :], ap[at:at + full * P].rearrange("(p i) -> p i", i=P))\
                      .then_inc(idx_loaded, 16)
                if E % P:
                    sp.dma_start(rows[full:full + 1, a, whole, 0:E % P],
                                 ap[at + full * P:E].rearrange("(p i) -> p i", p=1)).then_inc(idx_loaded, 16)
            whole = N // P
            sp.wait_ge(pads_set, 3)
            sp.dma_start(xs[:, 0:whole, :], x[0:whole * P, :].rearrange("(b p) k -> p b k", p=P))\
              .then_inc(x_loaded, 16)
            sp.dma_start(xs[0:N - whole * P, whole, :], x[whole * P:N, :]).then_inc(x_loaded, 16)
            sp.dma_start(w0s[:, :], w0).then_inc(w_loaded, 16)
            sp.dma_start(w1s[:, :, :], w1.rearrange("(a k) j -> k a j", a=2)).then_inc(w_loaded, 16)
            for i, a in enumerate((b1, w2.rearrange("k o -> (k o)"), gamma, beta)):
                sp.dma_start(vec[:, i, :], a.rearrange("(o k) -> o k", o=1).broadcast_to([P, D]))\
                  .then_inc(w_loaded, 16)
            sp.dma_start(b2s[:, :], b2.rearrange("(o k) -> o k", o=1).broadcast_to([P, 1]))\
              .then_inc(w_loaded, 16)

            def tables(b, p):
                sp.wait_ge(y_ready, b + 1)
                hold(sp, b)
                sp.dma_start(src_table[bass.ds(b * P, P), D:2 * D], yb[p][:, :]).then_inc(y_tabled[p], 16)
                sp.wait_ge(p_ready, b + 1)
                hold(sp, b)
                sp.dma_start(src_table[bass.ds(b * P, P), 0:D], Ps[p][:, :]).then_inc(p_tabled[p], 16)
                sp.wait_ge(q_ready, b + 1)
                hold(sp, b)
                sp.dma_start(tgt_table[bass.ds(b * P, P), :], Qs[p][:, :]).then_inc(q_tabled[p], 16)
            in_pairs(sp, tables, 0, NB)
            for p in range(2):
                sp.wait_ge(q_tabled[p], 16 * ((NB + 1 - p) // 2))

            def window(n, p):
                if not (is_static(n) and n < 2):
                    sp.wait_ge(ohT_ready, n - 1)
                    hold(sp, n)
                    sp.wait_ge(s_psum, (n - 1) * BPS)
                    hold(sp, n)
                first = load_four(ET.SP, base[0], n, N)
                for q in range(batches_in(n)):
                    sp.dma_start(qwin[p][q * QR:(q + 1) * QR, :], tgt_table[bass.ds(first[q], QR), :])\
                      .then_inc(win_loaded[p], 16)
                for q in range(batches_in(n)):
                    at = n * (BPS * BE) + q * BE
                    size = min(E - at, BE) if is_static(n) else BE
                    if size > 0:
                        sp.dma_start(dstb[p][q * QR:(q + 1) * QR, 0:size],
                                     dst[bass.ds(at, size)].rearrange("(o e) -> o e", o=1)
                                     .broadcast_to([QR, size])).then_inc(win_loaded[p], 16)
            in_pairs(sp, window, 0, SB - 2, 3)
            window(SB - 2, 1)
            window(SB - 1, 0)

            for g, (b0, b_end) in enumerate(GROUPS):
                sp.wait_ge(res_ready, g + 1)
                whole = min(b_end, N // P)
                if whole > b0:
                    sp.dma_start(out[b0 * P:whole * P, :].rearrange("(b p) k -> p b k", p=P),
                                 res[g % 2][:, 0:whole - b0, :]).then_inc(stored[g % 2], 16)
                if whole < b_end:
                    sp.dma_start(out[whole * P:N, :], res[g % 2][0:N - whole * P, whole - b0, :])\
                      .then_inc(stored[g % 2], 16)
            for p in range(min(2, len(GROUPS))):
                sp.wait_ge(stored[p], stores(p, len(GROUPS)))

        @block.gpsimd
        def _(g):
            nc.gpsimd.memset(rows[:, 0, E // (P * P):TB, :], NPAD).then_inc(pads_set, 1)
            nc.gpsimd.memset(rows[:, 1, E // (P * P):TB, :], N).then_inc(pads_set, 1)
            nc.gpsimd.memset(xs[:, NB - 1, :], 0.0).then_inc(pads_set, 1)
            nc.gpsimd.memset(ident[:, :], 0.0).then_inc(ident_zero, 1)
            nc.gpsimd.iota(iota[:, :], pattern=[[1, 512]], base=0, channel_multiplier=0,
                           allow_small_or_imprecise_dtypes=True)
            nc.gpsimd.memset(ones[:, :], 1.0)
            nc.gpsimd.memset(eps[:, :], LN_EPS)
            nc.gpsimd.memset(one[:, :], 1.0)
            nc.gpsimd.iota(place[:, :], pattern=[[0, 1]], base=0, channel_multiplier=1,
                           allow_small_or_imprecise_dtypes=True)
            nc.gpsimd.memset(U[0][:, :, 2 * D:2 * D + 2], 1.0)
            g.wait_ge(ident_zero, 1)
            nc.gpsimd.affine_select(out=ident[:, :], in_=ident[:, :], compare_op=ALU.not_equal, fill=1.0,
                                    base=0, pattern=[[-1, P]], channel_multiplier=1).then_inc(consts_set, 1)
            nc.gpsimd.memset(region[:, 0:NB * NPAD // 4], 0.0).then_inc(count_zeroed, 1)

            g.wait_ge(base_ready, 1)

            def take(n, p):
                nc.gpsimd.tensor_copy(now_g[p][:, :], meta[:, bass.ds(n, 1), LOW, :].rearrange(
                    "p o t -> p (o t)")).then_inc(now_g_ready, 1)
            take(0, 0)

            def lows(n, p):
                g.wait_ge(now_g_ready, n + 1)
                mine = [i for i in range(tiles_in(n)) if MAKER[i] == "G"]
                for i in mine:
                    if not (is_static(n) and n == 0):
                        g.wait_ge(tile_done, n * TPS + i - TPS + 1)
                        hold(g, n)
                    nc.gpsimd.tensor_scalar(L[:, i, :], iota[:, 0:P], now_g[p][:, i:i + 1], None,
                                            ALU.is_equal).then_inc(low_ready["G"], 1)
                    if i == mine[len(mine) // 2] and not (is_static(n) and n == SB - 1):
                        if not (is_static(n) and n == 0):
                            g.wait_ge(low_ready["G"], n * MAKER.count("G"))
                        take(n + 1, 1 - p)
            in_pairs(g, lows, 0, SB - 2)
            lows(SB - 2, 1)
            lows(SB - 1, 0)
            nc.gpsimd.memset(aggT[:, 0:NPAD], 0.0).then_inc(sums_zeroed, 1)

            def keep_y(b, p):
                g.wait_ge(y_ready, b + 1)
                nc.gpsimd.tensor_copy(blk(ys, b), yb[p][:, :]).then_inc(y_kept, 1)
            in_pairs(g, keep_y, 0, NB)

            for p in range(2):
                g.wait_ge(p_tabled[p], 16 * ((NB + 1 - p) // 2))
                g.wait_ge(y_tabled[p], 16 * ((NB + 1 - p) // 2))

            def gather(n, p):
                if not (is_static(n) and n < 2):
                    for q in range(BPS):
                        g.wait_ge(gathered[p * BPS + q], 32 * (n - p))
                nc.gpsimd.tensor_copy(inow[p][:, :], idx[:, bass.ds(n * TPS, TPS)]).then_inc(inow_ready, 1)
                g.wait_ge(inow_ready, n + 1)
                for i in range(tiles_in(n)):
                    q = i // TPB
                    if i % TPB == 0 and not (is_static(n) and n < 2):
                        g.wait_ge(agg_psum, (n - 2) * BPS + q + 1)
                        hold(g, n)
                    nc.gpsimd.indirect_dma_start(
                        out=G[:, p * TPS + i, :], out_offset=None, in_=src_table,
                        in_offset=bass.IndirectOffsetOnAxis(ap=inow[p][:, i:i + 1], axis=0))\
                        .then_inc(gathered[p * BPS + q], 16)
            gather(0, 0)
            gather(1, 1)
            in_pairs(g, gather, 2, SB - 2)
            gather(SB - 2, 1)
            gather(SB - 1, 0)

        @block.vector
        def _(dve):
            link = chained(dve, "prep", 0, 9)
            dve.wait_ge(pads_set, 2)
            dve.wait_ge(idx_loaded, 16 * 2 * (bool(E // (P * P)) + bool((E % (P * P)) // P) + bool(E % P)))
            r = rows[:, :, :, :].rearrange("p a b i -> p a (b i)")
            nc.vector.tensor_single_scalar(ints[:, 0, :], r[:, 0, :], 7, ALU.logical_shift_right)
            nc.vector.tensor_copy(rowf[:, 2, :], r[:, 1, :])
            link(nc.vector.tensor_single_scalar(ints[:, 1, :], r[:, 0, :], P - 1, ALU.bitwise_and))
            nc.vector.tensor_copy(rowf[:, 0:2, :], ints[:, :, :]).then_inc(rowf_ready, 1)
            dve.wait_ge(colf_ready, 3 * len(HALVES))
            for k in range(3):
                nc.vector.memset(base[k][0:1, 0:4], 0)
                link(nc.vector.memset(base[k][0:1, NBAT:NBAT + 4], 0))
                nc.vector.tensor_copy(base[k][0:1, k:NBAT + k], colf[0:1, 2, 0:T:TPB])
            dve.wait_ge(base_copied, 1)
            nc.vector.memset(shared_at[0:1, :], 0)
            nc.vector.memset(shared_is[:, :], 0.0)
            link(nc.vector.tensor_tensor(step_f[:, 1:NBAT], basebc[:, 1:NBAT], basebc[:, 0:NBAT - 1],
                                         ALU.subtract))
            nc.vector.tensor_scalar(shared_is[:, 1:NBAT], step_f[:, 1:NBAT], float(JW - 1), None, ALU.is_le)
            nc.vector.tensor_scalar(shared_at[0:1, 1:NBAT], step_f[0:1, 1:NBAT], float(JW - 1), 0.0,
                                    ALU.min, ALU.max)
            link(nc.vector.tensor_tensor(
                jT[:, :].rearrange("p (b t) -> p b t", t=TPB),
                colf[:, 2, 0:T].rearrange("p (b t) -> p b t", t=TPB),
                basebc[:, :].unsqueeze(2).broadcast_to([P, NBAT, TPB]), ALU.subtract))
            col = colf[:, :, 0:T].rearrange("p a (s t) -> p a s t", t=TPS)
            nc.vector.scalar_tensor_tensor(
                out=meta[:, :, 0, :], in0=col[:, 0], scalar=float(JW),
                in1=jT[:, :].rearrange("p (s t) -> p s t", t=TPS), op0=ALU.mult, op1=ALU.add)
            nc.vector.tensor_copy(meta[:, :, LOW, :], col[:, 1])
            nc.vector.tensor_copy(meta[:, :, HIGH, :], col[:, 0])
            link(nc.vector.scalar_tensor_tensor(out=idxf[:, :], in0=colf[:, 0, 0:T], scalar=float(P),
                                                in1=colf[:, 1, 0:T], op0=ALU.mult, op1=ALU.add))
            nc.vector.tensor_scalar_min(idx[:, :], idxf[:, :], float(NPAD - 1)).then_inc(base_ready, 1)
            dve.wait_ge(base_ready, 1)
            dve.wait_ge(consts_set, 1)

            def read_shared(b, at, q):
                if not (is_static(b) and b == 1):
                    dve.wait_ge(carried, b - 1)
                before = bank[(q - 1) % BPS][:, 0:CODES].rearrange("p (h j) -> p h j", j=JW)
                nc.vector.tensor_scalar(column[:, :, :], before[:, :, bass.ds(at, 1)],
                                        shared_is[:, bass.ds(b, 1)], None, ALU.mult).then_inc(column_read, 1)

            def add_shared(b, q):
                dve.wait_ge(tile_done, min((b + 1) * TPB, TILES) if is_static(b) else (b + 1) * TPB)
                dve.wait_ge(column_read, b)
                own = bank[q][:, 0:CODES].rearrange("p (h j) -> p h j", j=JW)[:, :, 0:1]
                nc.vector.tensor_tensor(own, own, column[:, :, :], ALU.add).then_inc(carried, 1)

            def take(n, p):
                nc.vector.tensor_copy(now[p][:, :, :], meta[:, bass.ds(n, 1), :, :].rearrange(
                    "p o a t -> p (o a) t")).then_inc(now_ready, 1)
            take(0, 0)

            def onehots(n, p):
                at = load_four(ET.DVE, shared_at, n, JW - 1)
                dve.wait_ge(now_ready, n + 1)
                for i in range(tiles_in(n)):
                    t = n * TPS + i
                    if i % NM == 0:
                        if not (is_static(n) and n == 0):
                            dve.wait_ge(tile_done, t - TPS + NM)
                        nc.vector.tensor_tensor(
                            H[i // NM][:, :, :], iota[:, 0:NB].unsqueeze(1).broadcast_to([P, NM, NB]),
                            now[p][:, HIGH, i:i + NM].unsqueeze(2).broadcast_to([P, NM, NB]),
                            ALU.is_equal).then_inc(hi_ready, 1)
                    if not (is_static(n) and t < NM):
                        dve.wait_ge(tile_done, t - NM + 1)
                    nc.vector.tensor_scalar(M[i % NM][:, :], iota[:, 0:CODES], now[p][:, CODE, i:i + 1], None,
                                            ALU.is_equal).then_inc(code_ready, 1)
                    if MAKER[i] == "D":
                        nc.vector.tensor_scalar(L[:, i, :], iota[:, 0:P], now[p][:, LOW, i:i + 1], None,
                                                ALU.is_equal).then_inc(low_ready["D"], 1)
                    if i % TPB == 1 and i + 1 < tiles_in(n) and not (is_static(n) and t < 2 * TPB):
                        add_shared(n * BPS + i // TPB - 1, (i // TPB - 1) % BPS)
                    if i % TPB == 2 and not (is_static(n) and t < TPB):
                        if is_static(n) and t < 2 * TPB:
                            dve.wait_ge(tile_done, TPB)
                        read_shared(n * BPS + i // TPB, at[i // TPB], i // TPB)
                    if i == TPS // 2 + 1 or (i == tiles_in(n) - 1 and i < TPS // 2 + 1):
                        if is_static(n) and n == SB - 1:
                            continue
                        if not (is_static(n) and n == 0):
                            dve.wait_ge(code_ready, n * TPS)
                            dve.wait_ge(low_ready["D"], n * MAKER.count("D"))
                        take(n + 1, 1 - p)
            in_pairs(dve, onehots, 0, SB - 2)
            onehots(SB - 2, 1)
            onehots(SB - 1, 0)
            for b in range((TILES - 3) // TPB, BATCHES):
                add_shared(b, b % BPS)
                if b < BATCHES - 1:
                    read_shared(b + 1, dve.value_load(shared_at[0:1, b + 1:b + 2], min_val=0, max_val=JW - 1),
                                (b + 1) % BPS)

            dve.wait_ge(tile_done, TILES)
            nc.vector.tensor_scalar_max(deg[:, :], bank[4][:, 0:NB], 1.0).then_inc(outdeg_ready, 1)
            dve.wait_ge(outroot_ready, 1)
            link(nc.vector.reciprocal(nout[:, :], rt[:, :]))
            nc.vector.tensor_scalar(su[:, :], nout[:, :], USCALE, None, ALU.mult)
            link(nc.vector.tensor_scalar(sh[:, :], nout[:, :], 0.5 * USCALE, None, ALU.mult))
            dve.wait_ge(x_loaded, 32)

            def start(b, p):
                link = chained(dve, "start", b * 1, 1)
                nc.vector.tensor_scalar(blk(hx, b), blk(xs, b), sh[:, bass.ds(b, 1)], None, ALU.mult)
                link(nc.vector.tensor_scalar(blk(U[0], b)[:, 0:D], blk(xs, b), su[:, bass.ds(b, 1)], None,
                                             ALU.mult))
                nc.vector.scalar_tensor_tensor(out=blk(U[0], b)[:, D:2 * D], in0=blk(xs, b),
                                               scalar=su[:, bass.ds(b, 1)], in1=blk(U[0], b)[:, 0:D],
                                               op0=ALU.mult, op1=ALU.subtract).then_inc(u_ready, 1)
            in_pairs(dve, start, 0, NB)

            def scaled_sums(k, b, p, factor, plus, link):
                ps = bank[2 * (k % 2) + p]
                link(nc.vector.scalar_tensor_tensor(
                    out=t1[p][:, :], in0=ps[:, D:2 * D], scalar=factor, in1=plus, op0=ALU.mult, op1=ALU.add))
                nc.vector.scalar_tensor_tensor(
                    out=t2[p][:, :], in0=ps[:, 0:D], scalar=factor, in1=t1[p][:, :], op0=ALU.mult,
                    op1=ALU.add).then_inc(hop_drained, 1)
                dve.wait_ge(hop_drained, k * NB + b + 1)

            def split(k, b, p, link):
                u = blk(U[(k + 1) % 2], b)
                link(nc.vector.tensor_copy(u[:, 0:D], t2[p][:, :]))
                nc.vector.tensor_tensor(u[:, D:2 * D], t2[p][:, :], u[:, 0:D], ALU.subtract)\
                  .then_inc(u_ready, 1)

            def hop0(b, p):
                link = chained(dve, "hop0", b * 4, 4)
                here = bass.ds(b, 1)
                dve.wait_ge(hop_psum, b + 1)
                nc.vector.tensor_scalar_max(indeg[:, here], bank[p][:, 2 * D:2 * D + 1], 1.0)\
                  .then_inc(indeg_ready, 1)
                dve.wait_ge(inroot_ready, b + 1)
                link(nc.vector.reciprocal(nin[:, here], irt[:, here]))
                nc.vector.tensor_scalar(c3[:, here], nin[:, here], 1.0 / USCALE, None, ALU.mult)
                link(nc.vector.scalar_tensor_tensor(out=c1[:, here], in0=nin[:, here], scalar=0.5,
                                                    in1=nout[:, here], op0=ALU.mult, op1=ALU.mult))
                scaled_sums(0, b, p, c1[:, here], blk(hx, b), link)
                split(0, b, p, link)
                link()

            def hop1(b, p):
                link = chained(dve, "hop1", b * 2, 2)
                dve.wait_ge(hop_psum, NB + b + 1)
                scaled_sums(1, b, p, c1[:, bass.ds(b, 1)], blk(hx, b), link)
                split(1, b, p, link)
                link()

            def hop2(b, p):
                link = chained(dve, "hop2", b * 4, 4)
                dve.wait_ge(hop_psum, 2 * NB + b + 1)
                scaled_sums(2, b, p, c3[:, bass.ds(b, 1)], blk(xs, b), link)
                dve.wait_ge(v_psum, b + 1)
                link(nc.vector.tensor_tensor(v[:, :], bank[5][:, 0:D], blk(xs, b), ALU.add))
                link(nc.vector.bn_stats(bns[:, :], v[:, :]))
                hold(dve, b)
                nc.vector.bn_aggr(mv[:, 0:2], bns[:, :]).then_inc(var_ready, 1)
                dve.wait_ge(dev_ready, b + 1)
                link(nc.vector.reciprocal(mv[:, 3:4], mv[:, 2:3]))
                if not (is_static(b) and b < 2):
                    dve.wait_ge(y_tabled[p], 8 * (b - p))
                    dve.wait_ge(y_kept, b - 1)
                nc.vector.tensor_scalar(yb[p][:, :], v[:, :], mv[:, 0:1], mv[:, 3:4], ALU.subtract, ALU.mult)\
                  .then_inc(y_ready, 1)
                dve.wait_ge(p_ready, b + 1)
                if not (is_static(b) and b < 2):
                    dve.wait_ge(q_tabled[p], 8 * (b - p))
                nc.vector.tensor_tensor(Qs[p][:, :], bank[6][:, D:2 * D], vec[:, B1, :], ALU.add)\
                  .then_inc(q_ready, 1)
                link()
            dve.wait_ge(w_loaded, 16 * 7)
            in_pairs(dve, hop0, 0, NB)
            in_pairs(dve, hop1, 0, NB)

            for q in range(BPS):
                nc.vector.tensor_scalar(rowid[q * QR:(q + 1) * QR, :], basebc[q * QR:(q + 1) * QR, q:NBAT:BPS],
                                        place[q * QR:(q + 1) * QR, 0:1], float(-q * QR), ALU.add, ALU.add)
            in_pairs(dve, hop2, 0, NB, 3)

            def scores(n, p, q):
                b = n * BPS + q
                m = tiles_of(b)
                dve.wait_ge(s_psum, b + 1)
                dve.wait_ge(gathered[p * BPS + q], 32 * (n - p) + 16 * m)
                nc.vector.tensor_tensor(
                    S[q % 2][:, 0:m, :], bank[q % 2][:, 0:m * P].rearrange("p (t k) -> p t k", t=m),
                    G[:, p * TPS + q * TPB:p * TPS + q * TPB + m, 0:D], ALU.add).then_inc(s_done, 1)
                dve.wait_ge(s_done, b + 1)
                for i in range(m):
                    z = nc.vector.scalar_tensor_tensor(
                        out=S[q % 2][:, i, :], in0=S[q % 2][:, i, :], scalar=0.0, in1=vec[:, W2, :],
                        op0=ALU.max, op1=ALU.mult, accum_out=zs[q % 2][:, i:i + 1])
                z.then_inc(z_ready, 1)
                dve.wait_ge(z_ready, b + 1)

            def weigh(n, p, q):
                b = n * BPS + q
                m = tiles_of(b)
                dve.wait_ge(w_ready, b + 1)
                if not (is_static(b) and b < 2):
                    dve.wait_ge(agg_psum, b - 1)
                nc.vector.tensor_tensor(
                    ohW[q % 2][:, 0:m, :], ohJ[p][:, q * TPB:q * TPB + m, :],
                    ws[q % 2][:, 0:m].unsqueeze(2).broadcast_to([P, m, JW]), ALU.mult).then_inc(ohw_ready, 1)

            def add_sums(b, q, first_target):
                dve.wait_ge(agg_psum, b + 1)
                if is_static(b) and b == 0:
                    dve.wait_ge(sums_zeroed, 1)
                else:
                    dve.wait_ge(agg_added, b)
                at = aggT[:, bass.ds(first_target, JW)]
                nc.vector.tensor_tensor(at, bank[2 + q % 2][:, 0:JW], at, ALU.add).then_inc(agg_added, 1)

            def attend(n, p):
                begin = is_static(n) and n == 0
                first = load_four(ET.DVE, base[2], n, N)
                dve.wait_ge(win_loaded[p], 16 * BPS * (n - p) + 32 * batches_in(n))
                if not (is_static(n) and n < 2):
                    dve.wait_ge(s_psum, (n - 1) * BPS)
                nc.vector.tensor_scalar(ohT[p][:, :], dstb[p][:, :], rowid[:, bass.ds(n, 1)], None,
                                        ALU.is_equal).then_inc(ohT_ready, 1)
                if not begin:
                    dve.wait_ge(ohw_ready, n * BPS - 1)
                nc.vector.tensor_tensor(
                    ohJ[p][:, :, :], iota[:, 0:JW].unsqueeze(1).broadcast_to([P, TPS, JW]),
                    jT[:, bass.ds(n * TPS, TPS)].unsqueeze(2).broadcast_to([P, TPS, JW]),
                    ALU.is_equal)
                for q in range(batches_in(n)):
                    scores(n, p, q)
                    if not (begin and q == 0):
                        weigh(*((n, p, q - 1) if q else (n - 1, 1 - p, BPS - 1)))
                    if not (begin and q < 2):
                        add_sums(n * BPS + q - 2, q, first[q])
            in_pairs(dve, attend, 0, SB - 2, 3)
            attend(SB - 2, 1)
            attend(SB - 1, 0)
            weigh(SB - 1, 0, (BATCHES - 1) % BPS)
            for b in (BATCHES - 2, BATCHES - 1):
                add_sums(b, b % BPS, dve.value_load(base[2][0:1, b + 2:b + 3], min_val=0, max_val=N))

            dve.wait_ge(y_kept, NB)
            done = [0]

            def last(ins):
                done[0] += 1
                ins.then_inc(chain["last"], 1)
                return done[0]
            for g, (b0, b_end) in enumerate(GROUPS):
                n = b_end - b0
                dve.wait_ge(att_psum, b_end)
                for i in range(n):
                    t = last(nc.vector.tensor_tensor(fa[:, i, :], bank[i][:, 0:D], ys[:, b0 + i, :], ALU.add))
                dve.wait_ge(chain["last"], t)
                for rnd in range(2):
                    source = fa if rnd == 0 else fb
                    for i in range(n):
                        t = last(nc.vector.bn_stats(fbn[:, i, :], source[:, i, :]))
                    dve.wait_ge(chain["last"], t)
                    for i in range(n):
                        z = nc.vector.bn_aggr(fmv[:, i, :], fbn[:, i, :])
                    z.then_inc(fvar_ready, 1)
                    dve.wait_ge(fdev_ready, 2 * g + rnd + 1)
                    t = last(nc.vector.reciprocal(frs[:, 0:n], fsd[:, 0:n]))
                    dve.wait_ge(chain["last"], t)
                    if rnd == 0:
                        for i in range(n):
                            t = last(nc.vector.tensor_scalar(fa[:, i, :], fa[:, i, :], fmv[:, i, 0:1],
                                                             frs[:, i:i + 1], ALU.subtract, ALU.mult))
                        dve.wait_ge(chain["last"], t)
                        t = last(nc.vector.tensor_tensor(fb[:, 0:n, :], fa[:, 0:n, :],
                                                         vec[:, GAMMA:GAMMA + 1, :].broadcast_to([P, n, D]),
                                                         ALU.mult))
                        dve.wait_ge(chain["last"], t)
                        t = last(nc.vector.tensor_tensor(fb[:, 0:n, :], fb[:, 0:n, :],
                                                         vec[:, BETA:BETA + 1, :].broadcast_to([P, n, D]),
                                                         ALU.add))
                        dve.wait_ge(chain["last"], t)
                        t = last(nc.vector.tensor_tensor(fb[:, 0:n, :], fb[:, 0:n, :], ys[:, b0:b_end, :],
                                                         ALU.add))
                        dve.wait_ge(chain["last"], t)
                    else:
                        if g >= 2:
                            dve.wait_ge(stored[g % 2], stores(g % 2, g))
                        for i in range(n):
                            z = nc.vector.tensor_scalar(res[g % 2][:, i, :], fb[:, i, :], fmv[:, i, 0:1],
                                                        frs[:, i:i + 1], ALU.subtract, ALU.mult)
                        z.then_inc(res_ready, 1)
                        dve.wait_ge(res_ready, g + 1)

        @block.tensor
        def _(pe):
            pe.wait_ge(rowf_ready, 1)
            pe.wait_ge(consts_set, 1)
            for a in range(3):
                for h, (k0, k1) in enumerate(HALVES):
                    for k in range(k0, k1):
                        z = nc.tensor.transpose(bank[2 * a + h][:, (k - k0) * P:(k - k0 + 1) * P],
                                                rowf[:, a, k * P:(k + 1) * P], ident[:, :])
                    z.then_inc(colf_psum, 1)
            pe.wait_ge(w_loaded, 16 * 7)
            nc.tensor.transpose(bank[7][:, 0:P], w0s[:, :], ident[:, :]).then_inc(w0T_psum, 1)
            pe.wait_ge(colf_ready, 3 * len(HALVES))
            nc.tensor.matmul(bank[6][:, 0:NBAT], ones[:, :], colf[0:1, 2, 0:T:TPB], start=True, stop=True)\
              .then_inc(base_psum, 1)

            def counts(n, p):
                begin = is_static(n) and n == 0
                for i in range(tiles_in(n)):
                    t, q = n * TPS + i, i // TPB
                    end = is_static(n) and t == TILES - 1
                    if i % NM == 0:
                        pe.wait_ge(hi_ready, n * (TPS // NM) + i // NM + 1)
                    if i % TPB == 0 and not begin:
                        pe.wait_ge(staged, n * BPS + q - BPS + 1)
                    pe.wait_ge(code_ready, t + 1)
                    pe.wait_ge(low_ready[MAKER[i]], made(n, i))
                    nc.tensor.matmul(bank[q][:, 0:CODES], L[:, i, :], M[i % NM][:, :],
                                     start=i % TPB == 0, stop=i % TPB == TPB - 1 or end)
                    nc.tensor.matmul(bank[4][:, 0:NB], L[:, i, :], H[i // NM][:, i % NM, :],
                                     start=begin and i == 0, stop=end).then_inc(tile_done, 1)
            in_pairs(pe, counts, 0, SB - 2)
            counts(SB - 2, 1)
            counts(SB - 1, 0)

            def node_step(step, b, p):
                if step == 0:
                    pe.wait_ge(hop_drained, 2 * NB + b + 1)
                    nc.tensor.transpose(bank[4][:, 0:P], t2[p][:, :], ident[:, :]).then_inc(x3T_psum, 1)
                elif step == 1:
                    pe.wait_ge(x3T_ready, b + 1)
                    nc.tensor.matmul(bank[5][:, 0:D], x3T[:, :], w0T[:, :], start=True, stop=True)\
                      .then_inc(v_psum, 1)
                elif step == 2:
                    pe.wait_ge(y_ready, b + 1)
                    nc.tensor.transpose(bank[7][:, 0:P], yb[p][:, :], ident[:, :]).then_inc(yT_psum, 1)
                else:
                    pe.wait_ge(yT_ready, b + 1)
                    if not (is_static(b) and b == 0):
                        pe.wait_ge(p_ready, b)
                        pe.wait_ge(q_ready, b)
                    nc.tensor.matmul(bank[6][:, 0:2 * D], yT[:, :],
                                     w1s[:, :, :].rearrange("k a j -> k (a j)"), start=True, stop=True)\
                      .then_inc(pq_psum, 1)

            def hop(k, b, p):
                begin = is_static(b) and b == 0
                width = 2 * D + 1 if k == 0 else 2 * D
                if b >= 2:
                    pe.wait_ge(hop_drained, k * NB + b - 1)
                after = [NB // 6, NB // 3, 2 * NB // 3, NB - 1]
                for h in range(NB):
                    if begin:
                        pe.wait_ge(u_ready, k * NB + h + 1)
                    z = nc.tensor.matmul(bank[2 * (k % 2) + p][:, 0:width],
                                         count[:, h, b * P:(b + 1) * P], U[k % 2][:, h, 0:width],
                                         start=h == 0, stop=h == NB - 1)
                    if h == NB - 1:
                        z.then_inc(hop_psum, 1)
                    for step in range(4):
                        if k == 2 and not begin and after[step] == h:
                            node_step(step, b - 1, 1 - p)
            pe.wait_ge(count_copied, BATCHES)
            for k in range(3):
                for b in range(NB):
                    hop(k, b, b % 2)
            for step in range(4):
                node_step(step, NB - 1, (NB - 1) % 2)

            def target_part(n, p, q):
                b = n * BPS + q
                if q == 0:
                    pe.wait_ge(ohT_ready, n + 1)
                if not (is_static(b) and b < 2):
                    pe.wait_ge(s_done, b - 1)
                for i in range(tiles_of(b)):
                    z = nc.tensor.matmul(bank[q % 2][:, i * P:(i + 1) * P],
                                         ohT[p][q * QR:(q + 1) * QR, i * P:(i + 1) * P],
                                         qwin[p][q * QR:(q + 1) * QR, :], start=True, stop=True)
                z.then_inc(s_psum, 1)

            def sums(n, p, q):
                b = n * BPS + q
                m = tiles_of(b)
                pe.wait_ge(ohw_ready, b + 1)
                if not (is_static(b) and b < 2):
                    pe.wait_ge(agg_added, b - 1)
                for i in range(m):
                    z = nc.tensor.matmul(bank[2 + q % 2][:, 0:JW], G[:, p * TPS + q * TPB + i, D:2 * D],
                                         ohW[q % 2][:, i, :], start=i == 0, stop=i == m - 1)
                z.then_inc(agg_psum, 1)

            def attend(n, p):
                for q in range(batches_in(n)):
                    target_part(n, p, q)
                    if not (is_static(n) and n == 0 and q < 2):
                        sums(*((n, p, q - 2) if q >= 2 else (n - 1, 1 - p, q + BPS - 2)))
            in_pairs(pe, attend, 0, SB - 2)
            attend(SB - 2, 1)
            attend(SB - 1, 0)
            for b in (BATCHES - 2, BATCHES - 1):
                sums(b // BPS, (b // BPS) % 2, b % BPS)

            pe.wait_ge(agg_added, BATCHES)
            for g, (b0, b_end) in enumerate(GROUPS):
                for b in range(b0, b_end):
                    if g:
                        pe.wait_ge(fvar_ready, 2 * g - 1)
                    nc.tensor.transpose(bank[b - b0][:, 0:P], aggT[:, b * P:(b + 1) * P], ident[:, :])\
                      .then_inc(att_psum, 1)

        @block.scalar
        def _(act):
            for a in range(3):
                for h, (k0, k1) in enumerate(HALVES):
                    act.wait_ge(colf_psum, a * len(HALVES) + h + 1)
                    nc.scalar.copy(colf[:, a, k0 * P:k1 * P], bank[2 * a + h][:, 0:(k1 - k0) * P])\
                      .then_inc(colf_ready, 1)
            act.wait_ge(base_psum, 1)
            nc.scalar.copy(basebc[:, :], bank[6][:, 0:NBAT]).then_inc(base_copied, 1)
            act.wait_ge(w0T_psum, 1)
            nc.scalar.mul(w0T[:, :], bank[7][:, 0:D], 0.5)

            act.wait_ge(base_ready, 1)
            act.wait_ge(consts_set, 1)

            def to_stage(b, q):
                if is_static(b) and b == BATCHES - 1:
                    act.wait_ge(carried, b)
                else:
                    act.wait_ge(column_read, b + 1)
                if not (is_static(b) and b < 2):
                    act.wait_ge(count_copied, b - 1)
                    hold(act, b)
                nc.scalar.activation(stage[q % 2][:, :, :],
                                     bank[q][:, 0:CODES].rearrange("p (h j) -> p h j", j=JW),
                                     ACT.Copy, saturate=True).then_inc(staged, 1)

            def to_window(b, q, to):
                act.wait_ge(staged, b + 1)
                if is_static(b) and b == 0:
                    act.wait_ge(count_zeroed, 1)
                else:
                    act.wait_ge(count_copied, b)
                nc.scalar.copy(count_bytes[:, :, bass.ds(to, JW)], stage[q % 2][:, :, :].bitcast(u8))\
                  .then_inc(count_copied, 1)

            def take(n, p):
                nc.scalar.copy(now_a[p][:, :], meta[:, bass.ds(n, 1), LOW, :].rearrange("p o t -> p (o t)"))\
                  .then_inc(now_a_ready, 1)
            take(0, 0)

            def lows(n, p, k):
                pair = [i for i in PAIRS[k] if i < tiles_in(n)]
                if not pair:
                    return
                before = n * len(PAIRS) + k
                if not (is_static(before) and before == 0):
                    act.wait_ge(low_ready["A"], before)
                for m, i in enumerate(pair):
                    nc.scalar.activation(away[:, m, :], iota[:, 0:P], ACT.Square, bias=now_a[p][:, i:i + 1],
                                         scale=-1.0).then_inc(away_ready, 1)
                act.wait_ge(away_ready, 2 * before + len(pair))
                if not (is_static(n) and n == 0):
                    act.wait_ge(tile_done, n * TPS + pair[-1] - TPS + 1)
                step = PAIRS[k][1] - PAIRS[k][0]
                nc.scalar.activation(L[:, pair[0]:pair[-1] + 1:step, :], away[:, 0:len(pair), :], ACT.Relu,
                                     bias=one[:, 0:1], scale=-1.0).then_inc(low_ready["A"], 1)

            def lows_and_counts(n, p):
                first = load_four(ET.Activation, base[2], n, N)
                act.wait_ge(now_a_ready, n + 1)
                lows(n, p, 0)
                for q in range(tiles_in(n) // TPB):
                    if not (is_static(n) and n == 0 and q == 0):
                        to_stage(n * BPS + q - 1, (q - 1) % BPS)
                        if not (is_static(n) and n == 0 and q == 1):
                            to_window(n * BPS + q - 2, (q - 2) % BPS, first[q])
                    if q == 0:
                        lows(n, p, 1)
                        if not (is_static(n) and n == SB - 1):
                            if not (is_static(n) and n == 0):
                                act.wait_ge(away_ready, n * 2 * len(PAIRS))
                            take(n + 1, 1 - p)
            in_pairs(act, lows_and_counts, 0, SB - 2)
            lows_and_counts(SB - 2, 1)
            lows_and_counts(SB - 1, 0)
            for b in range((TILES - TPB) // TPB - 1, BATCHES):
                if b + 1 < BATCHES:
                    to_stage(b + 1, (b + 1) % BPS)
                to_window(b, b % BPS, act.value_load(base[2][0:1, b + 2:b + 3], min_val=0, max_val=N))

            act.wait_ge(outdeg_ready, 1)
            nc.scalar.sqrt(rt[:, :], deg[:, :]).then_inc(outroot_ready, 1)

            def in_root(b, p):
                act.wait_ge(indeg_ready, b + 1)
                nc.scalar.sqrt(irt[:, bass.ds(b, 1)], indeg[:, bass.ds(b, 1)]).then_inc(inroot_ready, 1)
            in_pairs(act, in_root, 0, NB)

            def node(b, p):
                act.wait_ge(x3T_psum, b + 1)
                nc.scalar.copy(x3T[:, :], bank[4][:, 0:P]).then_inc(x3T_ready, 1)
                act.wait_ge(var_ready, b + 1)
                nc.scalar.activation(mv[:, 2:3], mv[:, 1:2], ACT.Sqrt, bias=eps[:, 0:1]).then_inc(dev_ready, 1)
                act.wait_ge(yT_psum, b + 1)
                nc.scalar.copy(yT[:, :], bank[7][:, 0:P]).then_inc(yT_ready, 1)
                act.wait_ge(pq_psum, b + 1)
                if not (is_static(b) and b < 2):
                    act.wait_ge(p_tabled[p], 8 * (b - p))
                nc.scalar.copy(Ps[p][:, :], bank[6][:, 0:D]).then_inc(p_ready, 1)
            in_pairs(act, node, 0, NB, 3)

            def sigmoids(n, p):
                for q in range(batches_in(n)):
                    b = n * BPS + q
                    m = tiles_of(b)
                    act.wait_ge(z_ready, b + 1)
                    if not (is_static(b) and b < 2):
                        act.wait_ge(ohw_ready, b - 1)
                    nc.scalar.activation(ws[q % 2][:, 0:m], zs[q % 2][:, 0:m], ACT.Sigmoid, bias=b2s[:, 0:1])\
                      .then_inc(w_ready, 1)
            in_pairs(act, sigmoids, 0, SB - 2)
            sigmoids(SB - 2, 1)
            sigmoids(SB - 1, 0)

            for g, (b0, b_end) in enumerate(GROUPS):
                for rnd in range(2):
                    act.wait_ge(fvar_ready, 2 * g + rnd + 1)
                    nc.scalar.activation(fsd[:, 0:b_end - b0], fmv[:, 0:b_end - b0, 1], ACT.Sqrt,
                                         bias=eps[:, 0:1]).then_inc(fdev_ready, 1)


_INS = ["x", "src", "dst", "L0_gnn_W", "L1_gnn_W1", "L1_gnn_b1", "L1_gnn_W2", "L1_gnn_b2",
        "L1_gnn_gamma", "L1_gnn_beta"]


def kernel(**inputs):
    import numpy as _np
    import concourse.bacc as _bacc
    from concourse import mybir as _mybir
    from concourse.bass_utils import run_bass_kernel_spmd as _run

    nc = _bacc.Bacc("TRN2", target_bir_lowering=False, num_devices=1)
    arrays, args = {}, []
    for name in _INS:
        a = _np.ascontiguousarray(inputs[name])
        arrays[f"in_{name}_dram"] = a
        args.append(nc.dram_tensor(f"in_{name}_dram", a.shape, _mybir.dt.from_np(a.dtype), kind="ExternalInput").ap())
    shape = inputs["x"].shape
    args.append(nc.dram_tensor("out_0_dram", shape, _mybir.dt.float32, kind="ExternalOutput").ap())
    gnn_kernel(nc, *args)
    r = _run(nc, [arrays], core_ids=[0])
    return r.results[0]["out_0_dram"]
```
